# Optimizing a Trainium2 kernel written in Bass

```python
import numpy as np
import jax
import jax.numpy as jnp

def _softmax(x, axis=-1):
    return jax.nn.softmax(x, axis=axis)

def _gelu(x):
    return jax.nn.gelu(x, approximate=True)

def _silu(x):
    return jax.nn.silu(x)

def _sigmoid(x):
    return jax.nn.sigmoid(x)

def _layernorm(x, axis=-1, eps=1e-05):
    m = jnp.mean(x, axis=axis, keepdims=True)
    v = jnp.var(x, axis=axis, keepdims=True)
    return (x - m) / jnp.sqrt(v + eps)

def _scatter_add(tgt, idx, src, axis=0):
    return tgt.at[idx].add(src)

def _segment_sum(src, seg, n):
    return jax.ops.segment_sum(src, seg, n)
kernel_name = 'mk_gnn_preln_d2_gnn_r64_ad88f1'

def setup_inputs(seed: int=0):
    np.random.seed(seed)
    _w = jnp.asarray

    def _rec_inputs():
        import jax
        import jax.numpy as jnp
        _gk = jax.random.key(seed)
        x = -0.000202 + 1 * jax.random.normal(jax.random.fold_in(_gk, 1), (100000, 128), jnp.float32)
        _s = jax.random.randint(jax.random.fold_in(_gk, 2), (12500,), 0, 100000, jnp.int32)
        _d = jax.random.randint(jax.random.fold_in(_gk, 3), (12500,), 0, 100000, jnp.int32)
        _loop = jnp.arange(100000, dtype=jnp.int32)
        src = jnp.concatenate([_s, _d, _loop])
        dst = jnp.concatenate([_d, _s, _loop])
        _o = jnp.argsort(dst, stable=True)
        src = src[_o]
        dst = dst[_o]
        return (x, src, dst)
    x, src, dst = _rec_inputs()

    def _L0_gnn_setup():
        import jax, jax.numpy as jnp
        import numpy as np
        N_NODES = 50000
        N_EDGES = 9375
        D_IN = 128
        D_OUT = 128
        key = jax.random.key(seed)
        k1, k2, k3, k4 = jax.random.split(key, 4)
        x = jax.random.normal(k1, (N_NODES, D_IN), dtype=jnp.float32)
        edge_index = jax.random.randint(k2, (2, N_EDGES), 0, N_NODES, dtype=jnp.int64)
        W1 = jax.random.normal(k3, (2 * D_IN, D_OUT), dtype=jnp.float32) * (1.0 / np.sqrt(2 * D_IN))
        b1 = jnp.zeros((D_OUT,), dtype=jnp.float32)
        W2 = jax.random.normal(k4, (D_OUT, D_OUT), dtype=jnp.float32) * (1.0 / np.sqrt(D_OUT))
        b2 = jnp.zeros((D_OUT,), dtype=jnp.float32)
        return {'x': x, 'edge_index': edge_index, 'W1': W1, 'b1': b1, 'W2': W2, 'b2': b2}
    _L0_gnn_all = _L0_gnn_setup()
    _L0_gnn_in = {k: v for k, v in _L0_gnn_all.items() if k in ('W1', 'b1', 'W2', 'b2')}
    del _L0_gnn_all

    def _L1_gnn_setup():
        import jax, jax.numpy as jnp
        import numpy as np
        NUM_STEPS = 1

        def _seg_mean(vals, idx, num_nodes):
            s = jax.ops.segment_sum(vals, idx, num_segments=num_nodes)
            cnt = jax.ops.segment_sum(jnp.ones((vals.shape[0],), vals.dtype), idx, num_segments=num_nodes)
            return s / jnp.maximum(cnt, 1.0)[:, None]

        def _gru_cell(a, h, w_ih, w_hh, b_ih, b_hh):
            gi = a @ w_ih.T + b_ih
            gh = h @ w_hh.T + b_hh
            H = h.shape[1]
            i_r, i_z, i_n = (gi[:, :H], gi[:, H:2 * H], gi[:, 2 * H:])
            h_r, h_z, h_n = (gh[:, :H], gh[:, H:2 * H], gh[:, 2 * H:])
            r = jax.nn.sigmoid(i_r + h_r)
            z = jax.nn.sigmoid(i_z + h_z)
            n = jnp.tanh(i_n + r * h_n)
            return (1.0 - z) * n + z * h
        key = jax.random.key(seed)
        ks = jax.random.split(key, 8)
        N, E, H = (100000, 10000, 128)
        sc = 1.0 / np.sqrt(H)
        feat = jax.random.normal(ks[0], (N, H), jnp.float32)
        src = jax.random.randint(ks[1], (E,), 0, N, jnp.int32)
        dst = jax.random.randint(ks[2], (E,), 0, N, jnp.int32)
        W_in = jax.random.normal(ks[3], (H, H), jnp.float32) * sc
        W_out = jax.random.normal(ks[4], (H, H), jnp.float32) * sc
        w_ih = jax.random.normal(ks[5], (3 * H, 2 * H), jnp.float32) * sc
        w_hh = jax.random.normal(ks[6], (3 * H, H), jnp.float32) * sc
        return {'feat': feat, 'src': src, 'dst': dst, 'W_in': W_in, 'b_in': jnp.zeros((H,), jnp.float32), 'W_out': W_out, 'b_out': jnp.zeros((H,), jnp.float32), 'w_ih': w_ih, 'w_hh': w_hh, 'b_ih': jnp.zeros((3 * H,), jnp.float32), 'b_hh': jnp.zeros((3 * H,), jnp.float32)}
    _L1_gnn_all = _L1_gnn_setup()
    _L1_gnn_in = {k: v for k, v in _L1_gnn_all.items() if k in ('W_in', 'b_in', 'W_out', 'b_out', 'w_ih', 'w_hh', 'b_ih', 'b_hh')}
    del _L1_gnn_all
    return {'x': x, 'src': src, 'dst': dst, 'L0_gnn_W1': _L0_gnn_in['W1'], 'L0_gnn_b1': _L0_gnn_in['b1'], 'L0_gnn_W2': _L0_gnn_in['W2'], 'L0_gnn_b2': _L0_gnn_in['b2'], 'L1_gnn_W_in': _L1_gnn_in['W_in'], 'L1_gnn_b_in': _L1_gnn_in['b_in'], 'L1_gnn_W_out': _L1_gnn_in['W_out'], 'L1_gnn_b_out': _L1_gnn_in['b_out'], 'L1_gnn_w_ih': _L1_gnn_in['w_ih'], 'L1_gnn_w_hh': _L1_gnn_in['w_hh'], 'L1_gnn_b_ih': _L1_gnn_in['b_ih'], 'L1_gnn_b_hh': _L1_gnn_in['b_hh']}

def reference(x, src, dst, L0_gnn_W1, L0_gnn_b1, L0_gnn_W2, L0_gnn_b2, L1_gnn_W_in, L1_gnn_b_in, L1_gnn_W_out, L1_gnn_b_out, L1_gnn_w_ih, L1_gnn_w_hh, L1_gnn_b_ih, L1_gnn_b_hh):
    import jax
    import jax.numpy as jnp

    def _L0_gnn_ref(x, edge_index, W1, b1, W2, b2):
        import jax, jax.numpy as jnp
        import numpy as np
        N_NODES = 50000
        N_EDGES = 9375
        D_IN = 128
        D_OUT = 128
        row, col = (edge_index[0], edge_index[1])
        x_col = x[col]
        feat = jnp.concatenate([x_col, x[row] - x_col], axis=-1)
        h = jax.nn.relu(feat @ W1 + b1)
        messages = h @ W2 + b2
        out = jax.ops.segment_max(messages, col, num_segments=x.shape[0])
        out = jnp.where(jnp.isneginf(out), jnp.zeros_like(out), out)
        return out

    def _L1_gnn_ref(feat, src, dst, W_in, b_in, W_out, b_out, w_ih, w_hh, b_ih, b_hh):
        import jax, jax.numpy as jnp
        import numpy as np
        NUM_STEPS = 1

        def _seg_mean(vals, idx, num_nodes):
            s = jax.ops.segment_sum(vals, idx, num_segments=num_nodes)
            cnt = jax.ops.segment_sum(jnp.ones((vals.shape[0],), vals.dtype), idx, num_segments=num_nodes)
            return s / jnp.maximum(cnt, 1.0)[:, None]

        def _gru_cell(a, h, w_ih, w_hh, b_ih, b_hh):
            gi = a @ w_ih.T + b_ih
            gh = h @ w_hh.T + b_hh
            H = h.shape[1]
            i_r, i_z, i_n = (gi[:, :H], gi[:, H:2 * H], gi[:, 2 * H:])
            h_r, h_z, h_n = (gh[:, :H], gh[:, H:2 * H], gh[:, 2 * H:])
            r = jax.nn.sigmoid(i_r + h_r)
            z = jax.nn.sigmoid(i_z + h_z)
            n = jnp.tanh(i_n + r * h_n)
            return (1.0 - z) * n + z * h
        N = feat.shape[0]
        h = feat
        for _ in range(NUM_STEPS):
            feat_in = h @ W_in.T + b_in
            feat_out = h @ W_out.T + b_out
            a_in = _seg_mean(feat_in[src], dst, N)
            a_out = _seg_mean(feat_out[dst], src, N)
            a = jnp.concatenate((a_in, a_out), axis=1)
            h = _gru_cell(a, h, w_ih, w_hh, b_ih, b_hh)
        return h
    edge_index = jnp.stack([src, dst])
    h = jnp.maximum(_layernorm(x, axis=-1), 0.0)
    x = x + _L0_gnn_ref(h, edge_index, L0_gnn_W1, L0_gnn_b1, L0_gnn_W2, L0_gnn_b2)
    h = jnp.maximum(_layernorm(x, axis=-1), 0.0)
    x = x + _L1_gnn_ref(h, src, dst, L1_gnn_W_in, L1_gnn_b_in, L1_gnn_W_out, L1_gnn_b_out, L1_gnn_w_ih, L1_gnn_w_hh, L1_gnn_b_ih, L1_gnn_b_hh)
    return x

_drawn_inputs = setup_inputs


def setup_inputs(seed=0):
    import zlib

    import numpy as np

    out = dict(_drawn_inputs(seed))
    spreads = {'L0_gnn_b1': (0.0, 0.1),
     'L0_gnn_b2': (0.0, 0.1),
     'L1_gnn_b_in': (0.0, 0.332),
     'L1_gnn_b_out': (0.0, 0.29),
     'L1_gnn_b_ih': (0.0, 0.289),
     'L1_gnn_b_hh': (0.0, 0.43)}
    factors = {}
    for name, (base, spread) in spreads.items():
        noise = np.random.default_rng([zlib.crc32(name.encode()), seed]).standard_normal(out[name].shape)
        drawn = base * np.exp(spread * noise) if base else spread * noise
        out[name] = jnp.asarray(drawn.astype(out[name].dtype))
    for name, factor in factors.items():
        out[name] = (out[name] * factor).astype(out[name].dtype)
    return out
```

```python
from contextlib import ExitStack

import concourse.bass as bass
from concourse import mybir

P = 128
D = 128
TILES = 3
GROUP = TILES * P
UN = 8
PEEL = 3
U = 8
BIG = 3.0e38
EPS = 1e-5

F32 = mybir.dt.float32
F16 = mybir.dt.float16
BF16 = mybir.dt.bfloat16
I32 = mybir.dt.int32
ALU = mybir.AluOpType
ACT = mybir.ActivationFunctionType
AX = mybir.AxisListType.X
RMAX = bass.bass_isa.ReduceOp.max


def sizes(n_nodes, n_edges):
    groups = -(-n_nodes // GROUP)
    cols = -(-n_edges // (P * 2 * U)) * 2 * U
    rounds = -(-n_edges // P)
    steps = max(2, -(-(groups + 2 * rounds + (PEEL + 1) * UN) // P))
    return groups, cols, rounds, steps


class Step:

    def __init__(self, i, c):
        self.i, self.c = i, c
        self.peeled = isinstance(i, int)

    @property
    def t(self):
        return self.i * UN + self.c

    def past(self, back):
        return not self.peeled or self.t >= back

    def slot(self, depth, back=0):
        return (self.c - back) % depth

    def count(self, per=1, back=0):
        return (self.i * UN + (self.c - back + 1)) * per

    def landed(self, turns, back=0, per=16):
        return (self.i * (UN // turns) + ((self.c - back) // turns + 1)) * per


def loop(eng, turns, stages):
    for n in range(PEEL * UN):
        for lag, stage in stages:
            if n >= lag:
                stage(Step(0, n - lag))
    with eng.Fori(0, turns) as i:
        for n in range(PEEL * UN, (PEEL + 1) * UN):
            for lag, stage in stages:
                stage(Step(i, n - lag))
    for n in range(max(lag for lag, _ in stages)):
        for lag, stage in stages:
            if n < lag:
                stage(Step(turns, PEEL * UN + n - lag))


def build(nc, n_nodes, n_edges, x, src, dst, weights, out):
    G, COLS, ROUNDS, TC = sizes(n_nodes, n_edges)
    CHUNKS = ROUNDS * G
    TMAX = P * TC
    PAD_KEY = 2 * n_nodes
    NO_LIST = float(1 << 20)

    lists = [nc.dram_tensor(f"lists_{by}", ((CHUNKS + 1) * P, 4), F16, kind="Internal").ap() for by in ("dst", "src")]
    step_dram = nc.dram_tensor("step_dram", (3, TMAX), I32, kind="Internal").ap()
    stepf_dram = nc.dram_tensor("stepf_dram", (3, TMAX), F32, kind="Internal").ap()

    x1_dram = nc.dram_tensor("x1_dram", ((G + 1) * GROUP, D), F32, kind="Internal").ap()
    h1_dram = nc.dram_tensor("h1_dram", ((G + 1) * GROUP, D), F32, kind="Internal").ap()

    ctx = ExitStack()
    with ctx:
        def sb(name, shape, dt):
            return ctx.enter_context(nc.sbuf_tensor(name, shape, dt))

        def ps(name, shape, dt=F32):
            return ctx.enter_context(nc.psum_tensor(name, shape, dt))

        def sem(name):
            return ctx.enter_context(nc.semaphore(name))

        ones_f = sb("ones_f", [P, P], F32)
        ones_b = sb("ones_b", [P, P], BF16)
        ident_f = sb("ident_f", [P, P], F32)
        before = sb("before", [P, P], BF16)
        not_before = sb("not_before", [P, P], BF16)
        iota_g = sb("iota_g", [P, G], F32)
        iota_c = sb("iota_c", [P, COLS], F32)
        iota_t = sb("iota_t", [P, TC], F32)
        sentinel = sb("sentinel", [P, G, 4], F16)

        looped = sb("looped", [P, 1], F32)
        rounds_i = sb("rounds_i", [P, 1], I32)
        n_turns = sb("n_turns", [P, 1], I32)

        with ExitStack() as prep:
            def tb(name, shape, dt):
                return prep.enter_context(nc.sbuf_tensor(name, shape, dt))
            planes = [tb(f"planes{n}", [P, 3, COLS], I32) for n in range(2)]
            nxt_i = tb("nxt_i", [P, COLS], I32)
            mask = tb("mask", [P, COLS], I32)
            zero_c = tb("zero_c", [P, COLS], I32)
            sf = tb("sf", [P, COLS], F32)
            df = tb("df", [P, COLS], F32)
            nf = tb("nf", [P, COLS], F32)
            flag = tb("flag", [P, COLS], F32)
            viol = tb("viol", [P, COLS], F32)
            cum = tb("cum", [P, COLS], F32)
            ones_c = tb("ones_c", [P, COLS], F32)
            key = tb("key", [P, 2, COLS], F32)
            quot_i = tb("quot_i", [P, 2, COLS], I32)
            quot = tb("quot", [P, 2, COLS], F32)
            loc = tb("loc", [P, 2, COLS], F32)
            over = tb("over", [P, 2, COLS], F32)
            entries = tb("entries", [P, 2, COLS, 4], F16)
            red = tb("red", [P, 8], F32)
            kept = tb("kept", [P, 2], F32)
            kept_i = tb("kept_i", [P, 8], I32)
            B = tb("B", [P, 4, G], BF16)
            prod = tb("prod", [P, 4, G], F32)
            kb8 = tb("kb8", [P, 2, 2, U], F32)
            rk8 = tb("rk8", [P, 2, 2, U], F32)
            ri8 = tb("ri8", [P, 3, 2, U], I32)
            rf8 = tb("rf8", [P, 2, 2, U], F32)
            pos8 = tb("pos8", [P, 2, 2, U], I32)
            ent8 = tb("ent8", [P, 2, 2, U, 4], F16)
            nb_i = tb("nb_i", [P, 2, G], I32)
            nb_f = tb("nb_f", [P, 2, G], F32)
            chunks = tb("chunks", [P, G], F32)
            ends = tb("ends", [P, G], F32)
            hit = tb("hit", [P, G], F32)
            tt = tb("tt", [P, 8, TC], F32)
            tf = tb("tf", [P, 3, TC], F32)
            ti = tb("ti", [P, 3, TC], I32)
            zero_b = tb("zero_b", [P, P], BF16)
            zero_g = tb("zero_g", [P, G], BF16)
            rank_ps = [prep.enter_context(nc.psum_tensor(f"rank_ps{k}", [P, 512], F32)) for k in range(2)]
            sum_ps = prep.enter_context(nc.psum_tensor("sum_ps", [P, 512], F32))

            s_load = sem("edges_loaded")
            s_const = sem("constants_ready")
            s_tmp = sem("pool_constants")
            s_v = sem("prep_vector")
            s_red = sem("partition_sums_ready")
            s_sum = sem("sums_ready")
            s_kept = sem("kept_counts_ready")
            s_kmax = sem("kept_maximum_ready")
            s_loops = sem("rank_trips_ready")
            s_fill = sem("lists_cleared")
            s_go = sem("second_scatter_started")
            s_rmax = sem("rounds_ready")
            s_tab = sem("step_table_ready")
            s_tabw = sem("step_table_stored")
            rank_sems = [dict(zero=sem(f"rank_sums_cleared{q}"), onehot=sem(f"onehot_ready{q}"),
                              rank=sem(f"ranks_summed{q}"), read=sem(f"rank_read{q}"),
                              pos=sem(f"positions_ready{q}"), scat=[sem(f"scattered{q}{h}") for h in range(2)],
                              last=sem(f"rank_sums_final{q}")) for q in range(2)]

            s_chain = [sem("rank_vector0"), sem("rank_vector1")]

            block = prep.enter_context(nc.Block())

            @block.sync
            def _(sp):
                sp.dma_start(planes[0][:, 0, :], src.rearrange("(p c) -> p c", p=P)).then_inc(s_load, 16)
                sp.dma_start(planes[0][:, 1, :], dst[0:P * COLS].rearrange("(p c) -> p c", p=P)).then_inc(s_load, 16)
                sp.dma_start(nxt_i[:, :], dst[1:P * COLS + 1].rearrange("(p c) -> p c", p=P)).then_inc(s_load, 16)
                sp.wait_ge(s_const, 1)
                for k in range(2):
                    sp.dma_start(lists[k][0:G * P, :].rearrange("(p g) e -> p g e", p=P), sentinel[:, :, :]).then_inc(s_fill, 16)
                    sp.dma_start(lists[k][CHUNKS * P:(CHUNKS + 1) * P, :], sentinel[:, 0, :]).then_inc(s_fill, 16)
                sp.wait_ge(s_rmax, 1)
                rmax = sp.value_load(kept_i[0:1, 2:3], min_val=1, max_val=ROUNDS)
                trips = sp.value_load(kept_i[0:1, 1:2], min_val=1, max_val=COLS // (2 * U))
                for h in range(2):
                    sp.wait_ge(rank_sems[0]["scat"][h], trips * (2 * U * 16))
                    sp.sem_inc(s_go, 1)
                with sp.If(rmax > 1):
                    with sp.Fori(1, rmax) as r:
                        for k in range(2):
                            sp.dma_start(lists[k][bass.ds(r * (G * P), G * P), :].rearrange("(p g) e -> p g e", p=P),
                                         sentinel[:, :, :]).then_inc(s_fill, 16)
                    for h in range(2):
                        sp.wait_ge(rank_sems[1]["scat"][h], trips * (2 * U * 16))
                        sp.sem_inc(s_go, 1)
                sp.wait_ge(s_tab, 1)
                sp.dma_start(step_dram.rearrange("k (p c) -> p k c", p=P), ti[:, :, :]).then_inc(s_tabw, 16)
                sp.dma_start(stepf_dram.rearrange("k (p c) -> p k c", p=P), tf[:, :, :]).then_inc(s_tabw, 16)
                sp.wait_ge(s_tabw, 32)

            @block.gpsimd
            def _(pool):
                nc.gpsimd.memset(sentinel[:, :, :], 0.0).then_inc(s_tmp, 1)
                pool.wait_ge(s_tmp, 1)
                nc.gpsimd.memset(sentinel[:, :, 2], 1000.0).then_inc(s_tmp, 1)
                pool.wait_ge(s_tmp, 2)
                nc.gpsimd.iota(iota_g[:, :], pattern=[[1, G]], base=0, channel_multiplier=0,
                               allow_small_or_imprecise_dtypes=True).then_inc(s_const, 1)
                nc.gpsimd.iota(iota_c[:, :], pattern=[[1, COLS]], base=0, channel_multiplier=0,
                               allow_small_or_imprecise_dtypes=True).then_inc(s_const, 1)
                nc.gpsimd.iota(iota_t[:, :], pattern=[[1, TC]], base=0, channel_multiplier=TC,
                               allow_small_or_imprecise_dtypes=True).then_inc(s_const, 1)
                nc.gpsimd.memset(ones_b[:, :], 1.0).then_inc(s_const, 1)
                nc.gpsimd.memset(ones_f[:, :], 1.0).then_inc(s_const, 1)
                nc.gpsimd.memset(ident_f[:, :], 0.0).then_inc(s_const, 1)
                pool.wait_ge(s_const, 6)
                nc.gpsimd.affine_select(out=ident_f[:, :], in_=ident_f[:, :], compare_op=ALU.not_equal, fill=1.0,
                                        base=0, pattern=[[-1, P]], channel_multiplier=1).then_inc(s_const, 1)
                nc.gpsimd.affine_select(out=before[:, :], in_=ones_b[:, :], compare_op=ALU.is_gt, fill=0.0,
                                        base=0, pattern=[[1, P]], channel_multiplier=-1).then_inc(s_const, 1)
                nc.gpsimd.affine_select(out=not_before[:, :], in_=ones_b[:, :], compare_op=ALU.is_ge, fill=0.0,
                                        base=0, pattern=[[-1, P]], channel_multiplier=1).then_inc(s_const, 1)
                nc.gpsimd.memset(zero_b[:, :], 0.0).then_inc(s_const, 1)
                pool.wait_ge(s_kept, 1)
                nc.gpsimd.partition_all_reduce(kept[:, 1:2], kept[:, 0:1], P, RMAX).then_inc(s_kmax, 1)
                pool.wait_ge(s_loops, 1)
                trips = pool.value_load(kept_i[0:1, 1:2], min_val=1, max_val=COLS // (2 * U))
                pool.wait_ge(s_fill, 64)

                def scatter(sems):
                    with pool.Fori(0, trips) as i:
                        for h in range(2):
                            pool.wait_ge(sems["pos"], 2 * i + h + 1)
                            pool.sem_inc(s_go, 1)
                            for k in range(2):
                                for u in range(U):
                                    nc.gpsimd.indirect_dma_start(
                                        out=lists[k][:, :], out_offset=bass.IndirectOffsetOnAxis(ap=pos8[:, h, k, u:u + 1], axis=0),
                                        in_=ent8[:, h, k, u, :], in_offset=None,
                                        bounds_check=CHUNKS * P - 1, oob_is_err=False).then_inc(sems["scat"][h], 16)

                scatter(rank_sems[0])
                pool.wait_ge(s_rmax, 1)
                rmax = pool.value_load(kept_i[0:1, 2:3], min_val=1, max_val=ROUNDS)
                with pool.If(rmax > 1):
                    pool.wait_ge(s_fill, rmax * 32 + 32)
                    pool.sem_inc(s_go, 1)
                    scatter(rank_sems[1])

            @block.tensor
            def _(pe):
                pe.wait_ge(s_const, 10)
                pe.wait_ge(s_red, 1)
                nc.tensor.matmul(sum_ps[:, 0:2], ones_f[:, :], red[:, 0:2], start=True, stop=True).then_inc(s_sum, 1)
                pe.wait_ge(s_loops, 1)
                trips = pe.value_load(kept_i[0:1, 1:2], min_val=1, max_val=COLS // (2 * U))

                def rank(sems):
                    N = 2 * U * 2
                    for k in range(2):
                        mm = nc.tensor.matmul(rank_ps[k][:, 0:G], zero_b[:, :], zero_g[:, :], start=True, stop=False, skip_group_check=True)

                    def first(n, i):
                        pe.wait_ge(sems["onehot"], i * N + n + 1)
                        nc.tensor.matmul(rank_ps[n % 2][:, 0:G], before[:, :], B[:, n % 4, :],
                                         start=False, stop=False, skip_group_check=True).then_inc(sems["rank"], 1)

                    def second(n, i):
                        pe.wait_ge(sems["read"], i * N + n + 1)
                        mm = nc.tensor.matmul(rank_ps[n % 2][:, 0:G], not_before[:, :], B[:, n % 4, :],
                                         start=False, stop=False, skip_group_check=True)
                        mm.then_inc(sems["last"], 1)

                    with pe.Fori(0, trips) as i:
                        first(0, i)
                        for n in range(1, N):
                            first(n, i)
                            second(n - 1, i)
                        second(N - 1, i)

                pe.wait_ge(rank_sems[0]["zero"], 1)
                rank(rank_sems[0])
                pe.wait_ge(s_rmax, 1)
                rmax = pe.value_load(kept_i[0:1, 2:3], min_val=1, max_val=ROUNDS)
                with pe.If(rmax > 1):
                    pe.wait_ge(rank_sems[1]["zero"], 1)
                    rank(rank_sems[1])

            @block.vector
            def _(v):
                done = [0]

                def link(ins):
                    done[0] += 1
                    ins.then_inc(s_v, 1)
                    v.wait_ge(s_v, done[0])

                V = nc.vector
                link(V.memset(ones_c[:, :], 1.0))
                link(V.memset(zero_c[:, :], 0))
                link(V.memset(entries[:, :, :, 3], 0.0))
                link(V.memset(zero_g[:, :], 0.0))
                v.wait_ge(s_load, 48)
                cur = planes[0]
                link(V.tensor_copy(sf[:, :], cur[:, 0, :]))
                link(V.tensor_copy(df[:, :], cur[:, 1, :]))
                link(V.tensor_copy(nf[:, :], nxt_i[:, :]))
                link(V.tensor_tensor(flag[:, :], sf[:, :], df[:, :], ALU.is_equal))
                link(V.tensor_tensor(viol[:, :], nf[:, :], df[:, :], ALU.not_equal))
                link(V.tensor_tensor(flag[:, :], flag[:, :], viol[:, :], ALU.mult))
                link(V.tensor_tensor(viol[:, :], nf[:, :], df[:, :], ALU.is_lt))
                link(V.tensor_reduce(red[:, 0:1], flag[:, :], AX, ALU.add))
                V.tensor_reduce(red[:, 1:2], viol[:, :], AX, ALU.add).then_inc(s_red, 1)
                v.wait_ge(s_sum, 1)
                link(V.tensor_scalar(red[:, 2:3], sum_ps[:, 0:1], float(n_nodes), None, ALU.is_equal))
                link(V.tensor_scalar(red[:, 3:4], sum_ps[:, 1:2], 0.0, None, ALU.is_equal))
                link(V.tensor_tensor(looped[:, :], red[:, 2:3], red[:, 3:4], ALU.mult))
                link(V.tensor_scalar(viol[:, :], df[:, :], 1.5 * n_nodes, None, ALU.is_lt))
                link(V.scalar_tensor_tensor(out=nf[:, :], in0=flag[:, :], scalar=looped[:, 0:1], in1=viol[:, :], op0=ALU.mult, op1=ALU.subtract))
                link(V.tensor_scalar(flag[:, :], nf[:, :], 1.0, None, ALU.add))
                link(V.tensor_tensor_scan(out=cum[:, :], data0=ones_c[:, :], data1=flag[:, :], initial=0.0, op0=ALU.mult, op1=ALU.add))
                link(V.scalar_tensor_tensor(out=cur[:, 2, :], in0=cum[:, :], scalar=-1.0, in1=nf[:, :], op0=ALU.mult, op1=ALU.mult))
                V.tensor_scalar(kept[:, 0:1], cum[:, COLS - 1:COLS], -1.0, float(COLS), ALU.mult, ALU.add).then_inc(s_kept, 1)
                bit = 1
                while bit < COLS:
                    new = planes[1] if cur is planes[0] else planes[0]
                    link(V.tensor_scalar(mask[:, :], cur[:, 2, :], bit, None, ALU.bitwise_and))
                    link(V.tensor_copy(new[:, :, :], cur[:, :, :]))
                    link(V.copy_predicated(new[:, 2, :], mask[:, :], zero_c[:, :]))
                    for q in range(3):
                        link(V.copy_predicated(new[:, q, 0:COLS - bit], mask[:, bit:COLS], cur[:, q, bit:COLS]))
                    cur, bit = new, bit * 2
                v.wait_ge(s_kmax, 1)
                link(V.tensor_scalar(kept_i[:, 0:1], kept[:, 1:2], float(2 * U - 1), None, ALU.add))
                link(V.tensor_scalar(kept_i[:, 3:4], kept_i[:, 0:1], 4, None, ALU.arith_shift_right))
                V.tensor_scalar(kept_i[:, 1:2], kept_i[:, 3:4], 1.0, None, ALU.max).then_inc(s_loops, 1)
                link(V.tensor_copy(key[:, 0, :], cur[:, 1, :]))
                link(V.tensor_copy(key[:, 1, :], cur[:, 0, :]))
                link(V.tensor_scalar(quot_i[:, :, :], key[:, :, :], 1.0 / GROUP, None, ALU.mult))
                link(V.tensor_copy(quot[:, :, :], quot_i[:, :, :]))
                link(V.scalar_tensor_tensor(out=loc[:, :, :], in0=quot[:, :, :], scalar=-float(GROUP), in1=key[:, :, :], op0=ALU.mult, op1=ALU.add))
                for lim, cmp, sign in ((0.0, ALU.is_lt, 1.0), (float(GROUP), ALU.is_ge, -1.0)):
                    link(V.tensor_scalar(over[:, :, :], loc[:, :, :], lim, None, cmp))
                    link(V.scalar_tensor_tensor(out=loc[:, :, :], in0=over[:, :, :], scalar=sign * GROUP, in1=loc[:, :, :], op0=ALU.mult, op1=ALU.add))
                    link(V.scalar_tensor_tensor(out=quot[:, :, :], in0=over[:, :, :], scalar=-sign, in1=quot[:, :, :], op0=ALU.mult, op1=ALU.add))
                link(V.tensor_scalar(over[:, 0, :], iota_c[:, :], kept[:, 0:1], NO_LIST, ALU.is_ge, ALU.mult))
                for k in range(2):
                    link(V.tensor_tensor(quot[:, k, :], quot[:, k, :], over[:, 0, :], ALU.add))
                    link(V.tensor_scalar(mask[:, :], cur[:, k, :], 8, None, ALU.arith_shift_right))
                    link(V.tensor_copy(entries[:, k, :, 0], mask[:, :]))
                    link(V.tensor_scalar(nxt_i[:, :], cur[:, k, :], 255, None, ALU.bitwise_and))
                    link(V.tensor_copy(entries[:, k, :, 1], nxt_i[:, :]))
                    link(V.tensor_scalar(entries[:, k, :, 2], loc[:, k, :], 1.0, None, ALU.add))
                trips = v.value_load(kept_i[0:1, 1:2], min_val=1, max_val=COLS // (2 * U))
                v.wait_ge(s_const, 10)

                def rank(sems, chain):
                    N = 2 * U * 2
                    PER = 9

                    def onehot(n, i):
                        h, u, k = n // (2 * U), n // 2 % U, n % 2
                        if n >= 4:
                            v.wait_ge(sems["last"], i * N + n - 3)
                        V.tensor_scalar(B[:, n % 4, :], iota_g[:, :], kb8[:, h, k, u:u + 1], None, ALU.is_equal).then_inc(sems["onehot"], 1)

                    def read(n, i):
                        h, u, k = n // (2 * U), n // 2 % U, n % 2
                        v.wait_ge(sems["rank"], i * N + n + 1)
                        V.tensor_tensor_reduce(prod[:, n % 4, :], B[:, n % 4, :], rank_ps[k][:, 0:G], 1.0, 0.0, ALU.mult, ALU.add,
                                               rk8[:, h, k, u:u + 1]).then_inc(sems["read"], 1)

                    with v.Fori(0, trips) as i:
                        for h in range(2):
                            v.wait_ge(sems["scat"][h], i * (2 * U * 16))
                            c0 = i * (2 * U) + h * U
                            V.tensor_copy(kb8[:, h, :, :], quot[:, :, bass.ds(c0, U)]).then_inc(chain, 1)
                            V.tensor_copy(ent8[:, h, :, :, :], entries[:, :, bass.ds(c0, U), :]).then_inc(chain, 1)
                        v.wait_ge(chain, i * (2 * PER) + 4)
                        v.wait_ge(sems["last"], i * N)
                        for n in range(2):
                            onehot(n, i)
                        for n in range(N):
                            read(n, i)
                            if n + 2 < N:
                                onehot(n + 2, i)
                            if n % (2 * U) == 2 * U - 1:
                                h = n // (2 * U)
                                at = [4 + 7 * h]

                                def step(ins):
                                    at[0] += 1
                                    ins.then_inc(chain, 1)
                                    v.wait_ge(chain, i * (2 * PER) + at[0])

                                v.wait_ge(sems["read"], i * N + n + 1)
                                step(V.tensor_copy(ri8[:, 0], rk8[:, h]))
                                step(V.tensor_scalar(ri8[:, 1], ri8[:, 0], 7, None, ALU.arith_shift_right))
                                step(V.tensor_scalar(ri8[:, 2], ri8[:, 0], P - 1, None, ALU.bitwise_and))
                                step(V.tensor_copy(rf8[:, 0], ri8[:, 1]))
                                step(V.scalar_tensor_tensor(out=ri8[:, 0], in0=rf8[:, 0], scalar=float(G), in1=kb8[:, h], op0=ALU.mult, op1=ALU.add))
                                step(V.tensor_scalar(ri8[:, 1], ri8[:, 0], 7, None, ALU.logical_shift_left))
                                step(V.tensor_tensor(pos8[:, h], ri8[:, 1], ri8[:, 2], ALU.bitwise_or))
                                V.tensor_copy(rf8[:, 1], rf8[:, 0]).then_inc(sems["pos"], 1)

                def counts():
                    link(V.tensor_copy(nb_f[:, 0, :], rank_ps[0][:, 0:G]))
                    link(V.tensor_copy(nb_f[:, 1, :], rank_ps[1][:, 0:G]))
                    link(V.tensor_scalar(nb_i[:, :, :], nb_f[:, :, :], float(P - 1), None, ALU.add))
                    link(V.tensor_scalar(nb_i[:, :, :], nb_i[:, :, :], 7, None, ALU.arith_shift_right))
                    link(V.tensor_copy(nb_f[:, :, :], nb_i[:, :, :]))
                    link(V.tensor_tensor(chunks[:, :], nb_f[:, 0, :], nb_f[:, 1, :], ALU.max))
                    link(V.tensor_scalar(chunks[:, :], chunks[:, :], 1.0, None, ALU.max))
                    link(V.tensor_reduce(red[:, 4:5], chunks[:, :], AX, ALU.max))

                V.memset(red[:, 5:6], 0.0).then_inc(rank_sems[0]["zero"], 1)
                rank(rank_sems[0], s_chain[0])
                v.wait_ge(rank_sems[0]["last"], trips * (4 * U))
                counts()
                V.tensor_copy(kept_i[:, 2:3], red[:, 4:5]).then_inc(s_rmax, 1)
                v.wait_ge(s_rmax, 1)
                rmax = v.value_load(kept_i[0:1, 2:3], min_val=1, max_val=ROUNDS)
                with v.If(rmax > 1):
                    for h in range(2):
                        v.wait_ge(rank_sems[0]["scat"][h], trips * (2 * U * 16))
                    V.memset(red[:, 5:6], 0.0).then_inc(rank_sems[1]["zero"], 1)
                    rank(rank_sems[1], s_chain[1])
                link(V.tensor_tensor_scan(out=ends[:, :], data0=ones_c[:, 0:G], data1=chunks[:, :], initial=0.0, op0=ALU.mult, op1=ALU.add))
                for c in range(TC):
                    link(V.tensor_scalar(hit[:, :], ends[:, :], iota_t[:, c:c + 1], None, ALU.is_le))
                    link(V.tensor_reduce(tt[:, 0, c:c + 1], hit[:, :], AX, ALU.add))
                    link(V.tensor_tensor_reduce(prod[:, 0, :], hit[:, :], chunks[:, :], 1.0, 0.0, ALU.mult, ALU.add, tt[:, 1, c:c + 1]))
                link(V.tensor_tensor(tt[:, 2, :], iota_t[:, :], tt[:, 1, :], ALU.subtract))
                link(V.tensor_scalar(tt[:, 4, :], tt[:, 0, :], float(GROUP), None, ALU.mult))
                link(V.tensor_scalar(tf[:, 0, :], tt[:, 0, :], float(GROUP), -1.0, ALU.mult, ALU.add))
                link(V.tensor_scalar(tf[:, 1, :], tt[:, 2, :], 0.0, None, ALU.is_gt))
                link(V.tensor_scalar(tf[:, 2, :], tt[:, 2, :], 0.0, -BIG, ALU.is_le, ALU.mult))
                link(V.scalar_tensor_tensor(out=tt[:, 6, :], in0=tt[:, 2, :], scalar=float(G), in1=tt[:, 0, :], op0=ALU.mult, op1=ALU.add))
                link(V.tensor_scalar(tt[:, 7, :], tt[:, 0, :], float(G - 1), None, ALU.is_gt))
                link(V.tensor_scalar(tt[:, 2, :], tt[:, 6, :], -1.0, float(CHUNKS), ALU.mult, ALU.add))
                link(V.tensor_tensor(tt[:, 2, :], tt[:, 2, :], tt[:, 7, :], ALU.mult))
                link(V.tensor_tensor(tt[:, 6, :], tt[:, 6, :], tt[:, 2, :], ALU.add))
                link(V.tensor_copy(ti[:, 0, :], tt[:, 4, :]))
                link(V.tensor_copy(rounds_i[:, :], red[:, 4:5]))
                link(V.tensor_copy(ti[:, 1, :], tt[:, 6, :]))
                link(V.tensor_scalar(kept_i[:, 4:5], ends[:, G - 1:G], float(UN), None, ALU.add))
                link(V.tensor_scalar(kept_i[:, 5:6], kept_i[:, 4:5], 3, None, ALU.arith_shift_right))
                link(V.tensor_scalar(n_turns[:, 0:1], kept_i[:, 5:6], -float(PEEL), None, ALU.add))
                V.memset(ti[:, 2, :], 0).then_inc(s_tab, 1)

        layer_max(nc, locals())
        layer_gru(nc, locals())


def layer_max(nc, env):
    G, TMAX, n_nodes, weights, lists = (env[k] for k in ("G", "TMAX", "n_nodes", "weights", "lists"))
    x, x1_dram, h1_dram, step_dram, stepf_dram = (env[k] for k in ("x", "x1_dram", "h1_dram", "step_dram", "stepf_dram"))
    ones_f, ones_b, ident_f, n_turns, looped, rounds_i = (env[k] for k in ("ones_f", "ones_b", "ident_f", "n_turns", "looped", "rounds_i"))
    NPAD = (G + 1) * GROUP
    max_turns = TMAX // UN - PEEL

    with ExitStack() as ctx:
        def sb(name, shape, dt=F32):
            return ctx.enter_context(nc.sbuf_tensor(name, shape, dt))

        def ps(name, shape, dt=F32):
            return ctx.enter_context(nc.psum_tensor(name, shape, dt))

        def sem(name):
            return env["ctx"].enter_context(nc.semaphore(name))

        w1a = sb("w1a", [P, D])
        w1b = sb("w1b", [P, D])
        w2 = sb("w2", [P, D])
        b1 = sb("b1", [P, 1])
        b2 = sb("b2", [P, 1])
        w1d = sb("w1d", [P, D])
        b1_own = sb("b1_own", [P, 1])
        no_own = sb("no_own", [P, 1])
        gap = sb("gap", [P, 1])
        eps = sb("eps", [P, 1])
        rounds_f = sb("rounds_f", [P, 1])
        general_f = sb("general_f", [P, 1])
        looped_i = sb("looped_i", [P, 1], I32)
        general_i = sb("general_i", [P, 1], I32)
        step_row = sb("step_row", [1, 2, TMAX], I32)
        step_f = sb("step_f", [P, 3, TMAX])
        ones_h = sb("ones_h", [P, P], F16)
        ident_h = sb("ident_h", [P, P], F16)
        half_before = sb("half_before", [P, P], F16)
        iota_n = sb("iota_n", [P, P + 2])
        iota_loc = sb("iota_loc", [P, TILES, P])

        ent = sb("ent", [P, UN, 4], F16)
        rep = sb("rep", [P, 2, P], F16)
        junk = sb("junk", [P, 2, P])
        rank = sb("rank", [P, 2])
        place = sb("place", [P, 2, P + 2], F16)
        dplace = sb("dplace", [P, 2, P + 1], F16)
        sorted4 = sb("sorted4", [P, 2, 4])
        reset = sb("reset", [P, UN, P])
        idx = sb("idx", [P, 4, 2], I32)
        last_loc = sb("last_loc", [P, UN, 1])
        carry = sb("carry", [P, 1])
        x3 = sb("x3", [P, UN, TILES, D])
        xg = sb("xg", [P, 4, 2, D])
        stats = sb("stats", [P, 2, 5, 6])
        mv = sb("mv", [P, 2, 5, 2])
        std = sb("std", [P, 2, 5])
        rs = sb("rs", [P, 4, 5])
        nm = sb("nm", [P, 4, 5])
        h = sb("h", [P, 2, 5, D])
        hT = sb("hT", [P, 2, 5 * P])
        hid = sb("hid", [P, 4, 5 * P])
        runmax = sb("runmax", [P, 2, P])
        reached = sb("reached", [P, 2, P])
        gain = sb("gain", [P, 2, P])
        part = sb("part", [P, 2, 3, D], BF16)
        rest = sb("rest", [P, 2, D])
        onehot = sb("onehot", [P, 2, GROUP], BF16)
        resT = sb("resT", [P, 2, GROUP])
        absent = sb("absent", [P, GROUP])
        found = sb("found", [P, GROUP])
        kept = sb("kept_max", [P, 2, GROUP])
        raw = sb("raw", [P, 2, GROUP])
        x1s = sb("x1s", [P, 4, GROUP])
        stats1 = sb("stats1", [P, 2, 3, 6])
        mv1 = sb("mv1", [P, 2, 3, 2])
        std1 = sb("std1", [P, 2, 3])
        rs1 = sb("rs1", [P, 2, 3])
        nm1 = sb("nm1", [P, 2, 3])
        h1s = sb("h1s", [P, 4, GROUP])

        ps_k = ps("ps_k", [P, 512])
        ps_t = ps("ps_t", [P, 512])
        ps_e = ps("ps_e", [P, 512])
        ps_h = ps("ps_h", [P, 512])
        ps_m = ps("ps_m", [P, 512])
        ps_g = ps("ps_g", [P, 512])
        ps_x = ps("ps_x", [P, 512])
        ps_o = ps("ps_o", [P, 512])

        names = ("weights const prep rep key rank pe dp sorted srt idx bn mv std rs h tn te hT hidep hide msge "
                 "scan most gain scT hi r1 mid lo oh seen t1 t2 cont ext res O x1 bn1 mv1 std1 rs1 h1 raw carry go").split()
        S = {n: sem(f"a_{n}") for n in names}
        d_ent, d_x, d_gat = ([sem(f"a_{n}{q}") for q in range(4)] for n in ("ent_in", "x_in", "gathered"))
        d_x1, d_h1 = ([sem(f"a_{n}{q}") for q in range(2)] for n in ("x1_out", "h1_out"))

        block = ctx.enter_context(nc.Block())

        def turns_of(eng):
            return eng.value_load(n_turns[0:1, 0:1], min_val=1, max_val=max_turns)

        def after(eng, name, st, per=1, back=0):
            if st.past(back):
                eng.wait_ge(S[name], st.count(per, back))

        def landed(eng, sems, st, back=0, per=16):
            if st.past(back):
                eng.wait_ge(sems[st.slot(len(sems), back)], st.landed(len(sems), back, per))

        @block.sync
        def _(sp):
            for tile, src in ((w1a, weights["W1"][0:D, :]), (w1b, weights["W1"][D:2 * D, :]), (w2, weights["W2"]),
                              (b1, weights["b1"].rearrange("(p o) -> p o", o=1)), (b2, weights["b2"].rearrange("(p o) -> p o", o=1))):
                sp.dma_start(tile[:, :], src).then_inc(S["weights"], 16)
            sp.dma_start(step_row[:, :, :], step_dram[0:2, :].rearrange("(o k) t -> o k t", o=1)).then_inc(S["weights"], 16)
            sp.dma_start(step_f[:, :, :], stepf_dram.rearrange("(o k) t -> o k t", o=1).broadcast_to([P, 3, TMAX])).then_inc(S["weights"], 16)
            sp.wait_ge(S["weights"], 7 * 16)
            turns = turns_of(sp)

            def entries_in(st):
                chunk = sp.value_load(step_row[0:1, 1, bass.ds(st.t, 1)], min_val=0, max_val=env["CHUNKS"])
                after(sp, "rep", st, back=4)
                sp.sem_inc(S["go"], 1)
                after(sp, "sorted", st, back=UN)
                sp.dma_start(ent[:, st.slot(UN), :], lists[0][bass.ds(chunk * P, P), :]).then_inc(d_ent[st.slot(4)], 16)

            def x_in(st):
                base = sp.value_load(step_row[0:1, 0, bass.ds(st.t, 1)], min_val=0, max_val=NPAD - GROUP)
                after(sp, "x1", st, back=UN)
                sp.dma_start(x3[:, st.slot(UN), :, :],
                             x[bass.ds(base, GROUP), :].rearrange("(p t) d -> p t d", t=TILES)).then_inc(d_x[st.slot(4)], 16)

            def rows_out(st):
                base = sp.value_load(step_row[0:1, 0, bass.ds(st.t, 1)], min_val=0, max_val=NPAD - GROUP)
                for name, sems, tile, dram in (("x1", d_x1, x1s, x1_dram), ("h1", d_h1, h1s, h1_dram)):
                    after(sp, name, st, per=1 if name == "x1" else 3)
                    landed(sp, sems, st, back=1)
                    sp.dma_start(dram[bass.ds(base, GROUP), :].rearrange("(p t) d -> p (t d)", t=TILES),
                                 tile[:, st.slot(4), :]).then_inc(sems[st.slot(2)], 16)

            loop(sp, turns, [(0, entries_in), (6, x_in), (15, rows_out)])
            for sems in (d_x1, d_h1):
                landed(sp, sems, Step(turns, PEEL * UN - 1))
                sp.sem_inc(S["carry"], 1)

        @block.gpsimd
        def _(pool):
            G_ = nc.gpsimd
            G_.iota(iota_n[:, :], pattern=[[1, P + 2]], base=-1, channel_multiplier=0, allow_small_or_imprecise_dtypes=True).then_inc(S["const"], 1)
            G_.iota(iota_loc[:, :, :], pattern=[[1, TILES], [TILES, P]], base=1, channel_multiplier=0,
                    allow_small_or_imprecise_dtypes=True).then_inc(S["const"], 1)
            G_.memset(ones_h[:, :], 1.0).then_inc(S["const"], 1)
            G_.memset(eps[:, :], EPS).then_inc(S["const"], 1)
            G_.memset(half_before[:, :], -0.5).then_inc(S["const"], 1)
            G_.memset(kept[:, :, :], 0.0).then_inc(S["const"], 1)
            pool.wait_ge(S["const"], 6)
            G_.affine_select(out=half_before[:, :], in_=half_before[:, :], compare_op=ALU.is_gt, fill=0.0, base=0,
                             pattern=[[-1, P]], channel_multiplier=1).then_inc(S["const"], 1)
            G_.affine_select(out=ident_h[:, :], in_=ones_h[:, :], compare_op=ALU.is_equal, fill=0.0, base=0,
                             pattern=[[-1, P]], channel_multiplier=1).then_inc(S["const"], 1)
            turns = turns_of(pool)

            def gather(st):
                after(pool, "idx", st, per=3)
                after(pool, "h", st, per=5, back=4)
                pool.sem_inc(S["go"], 1)
                for q in range(2):
                    G_.indirect_dma_start(out=xg[:, st.slot(4), q, :], out_offset=None, in_=x[:, :],
                                          in_offset=bass.IndirectOffsetOnAxis(ap=idx[:, st.slot(4), q:q + 1], axis=0)
                                          ).then_inc(d_gat[st.slot(4)], 16)

            def low_part(st):
                after(pool, "mid", st)
                after(pool, "ext", st, back=2)
                G_.tensor_tensor(part[:, st.slot(2), 2, :], rest[:, st.slot(2), :], part[:, st.slot(2), 1, :], ALU.subtract).then_inc(S["lo"], 1)

            loop(pool, turns, [(6, gather), (11, low_part)])

        @block.scalar
        def _(act):
            A = nc.scalar
            turns = turns_of(act)
            act.wait_ge(S["weights"], 7 * 16)
            act.wait_ge(S["const"], 8)
            act.wait_ge(S["prep"], 9)
            general = act.value_load(general_i[0:1, 0:1], min_val=0, max_val=1)

            def deviation(st):
                after(act, "mv", st, per=5)
                after(act, "rs", st, per=2, back=2)
                A.activation(std[:, st.slot(2), :], mv[:, st.slot(2), :, 1], ACT.Sqrt, bias=eps[:, :]).then_inc(S["std"], 1)

            def normalize(st):
                after(act, "rs", st, per=2)
                after(act, "te", st, back=2)
                for q in range(5):
                    rows = x3[:, st.slot(UN), q, :] if q < 3 else xg[:, st.slot(4), q - 3, :]
                    A.activation(h[:, st.slot(2), q, :], rows, ACT.Relu, bias=nm[:, st.slot(4), q:q + 1],
                                 scale=rs[:, st.slot(4), q:q + 1]).then_inc(S["h"], 1)

            def columns(st):
                after(act, "tn", st)
                after(act, "hidep", st, back=2)
                A.copy(hT[:, st.slot(2), 0:4 * P], ps_t[:, :]).then_inc(S["hT"], 1)
                after(act, "te", st)
                A.copy(hT[:, st.slot(2), 4 * P:5 * P], ps_e[:, 0:P]).then_inc(S["hT"], 1)

            def hidden(st):
                after(act, "hidep", st)
                after(act, "ext", st, back=4)
                A.activation(hid[:, st.slot(4), 0:4 * P], ps_h[:, :], ACT.Relu, bias=b1_own[:, :], scale=looped[:, :]).then_inc(S["hide"], 1)
                A.activation(hid[:, st.slot(4), 4 * P:5 * P], ps_e[:, P:2 * P], ACT.Relu, bias=b1[:, :]).then_inc(S["hide"], 1)

            def high_part(st):
                after(act, "scT", st)
                after(act, "ext", st, back=2)
                A.copy(part[:, st.slot(2), 0, :], ps_g[:, 0:P]).then_inc(S["hi"], 1)

            def middle_part(st):
                after(act, "r1", st)
                A.copy(part[:, st.slot(2), 1, :], rest[:, st.slot(2), :]).then_inc(S["mid"], 1)

            def results(st):
                after(act, "ext", st)
                after(act, "O", st, back=2)
                A.activation(resT[:, st.slot(2), :], ps_x[:, 0:GROUP], ACT.Identity, bias=b2[:, :]).then_inc(S["res"], 1)
                act.sem_inc(S["go"], 1)
                with act.If(general > 0):
                    after(act, "seen", st)
                    after(act, "t2", st, back=1)
                    A.activation(absent[:, :], ps_o[:, 0:GROUP], ACT.Identity, bias=no_own[:, :], scale=gap[:, :]).then_inc(S["t1"], 1)

            def deviation1(st):
                after(act, "mv1", st, per=3)
                after(act, "rs1", st, per=2, back=2)
                A.activation(std1[:, st.slot(2), :], mv1[:, st.slot(2), :, 1], ACT.Sqrt, bias=eps[:, :]).then_inc(S["std1"], 1)

            def normalize1(st):
                after(act, "rs1", st, per=2)
                landed(act, d_h1, st, back=4)
                for q in range(3):
                    A.activation(h1s[:, st.slot(4), q * D:(q + 1) * D], x1s[:, st.slot(4), q * D:(q + 1) * D], ACT.Relu,
                                 bias=nm1[:, st.slot(2), q:q + 1], scale=rs1[:, st.slot(2), q:q + 1]).then_inc(S["h1"], 1)

            loop(act, turns, [(11, high_part), (8, deviation), (14, deviation1), (9, columns), (12, results), (8, normalize), (11, middle_part),
                              (14, normalize1), (9, hidden)])

        @block.tensor
        def _(pe):
            T = nc.tensor
            turns = turns_of(pe)
            pe.wait_ge(S["weights"], 7 * 16)
            pe.wait_ge(S["const"], 8)
            pe.wait_ge(S["prep"], 9)
            general = pe.value_load(general_i[0:1, 0:1], min_val=0, max_val=1)

            def keys(st):
                after(pe, "rep", st)
                after(pe, "srt", st, per=2, back=1)
                T.matmul(ps_k[:, 0:P], rep[:, st.slot(2), :], ident_h[:, :], start=True, stop=False)
                T.matmul(ps_k[:, 0:P], ident_h[:, :], half_before[:, :], start=False, stop=True).then_inc(S["key"], 1)

            def sort(st):
                after(pe, "dp", st)
                landed(pe, d_ent, st)
                after(pe, "rank", st)
                s2, e4 = st.slot(2), ent[:, st.slot(UN), :]
                T.matmul(ps_k[:, 256:259], place[:, s2, 1:P + 1], e4[:, 0:3], start=True, stop=True)
                T.matmul(ps_k[:, 259:260], dplace[:, s2, 1:P + 1], e4[:, 2:3], start=True, stop=True)
                T.matmul(ps_k[:, P:2 * P], rep[:, s2, :], dplace[:, s2, 0:P], start=True, stop=True).then_inc(S["sorted"], 1)

            def turn_rows(st):
                after(pe, "h", st, per=5)
                after(pe, "hT", st, per=2, back=1)
                for q in range(4):
                    mm = T.transpose(ps_t[:, q * P:(q + 1) * P], h[:, st.slot(2), (0, 1, 2, 4)[q], :], ident_f[:, :])
                mm.then_inc(S["tn"], 1)
                after(pe, "hide", st, per=2, back=1)
                T.transpose(ps_e[:, 0:P], h[:, st.slot(2), 3, :], ident_f[:, :]).then_inc(S["te"], 1)

            def mlp(st):
                after(pe, "hT", st, per=2)
                after(pe, "hide", st, per=2, back=1)
                s2 = st.slot(2)
                T.matmul(ps_h[:, :], w1a[:, :], hT[:, s2, 0:4 * P], start=True, stop=True)
                T.matmul(ps_e[:, P:2 * P], w1d[:, :], hT[:, s2, 3 * P:4 * P], start=True, stop=False)
                T.matmul(ps_e[:, P:2 * P], w1b[:, :], hT[:, s2, 4 * P:5 * P], start=False, stop=True).then_inc(S["hidep"], 1)

            def messages(st):
                after(pe, "hide", st, per=2)
                after(pe, "gain", st, back=1)
                T.matmul(ps_m[:, 0:2 * P], w2[:, :], hid[:, st.slot(4), 3 * P:5 * P], start=True, stop=True).then_inc(S["msge"], 1)

            def turn_gains(st):
                after(pe, "gain", st)
                after(pe, "hi", st, back=1)
                after(pe, "r1", st, back=1)
                T.transpose(ps_g[:, 0:P], gain[:, st.slot(2), :], ident_f[:, :]).then_inc(S["scT"], 1)

            def spread(st):
                after(pe, "lo", st)
                after(pe, "oh", st)
                after(pe, "res", st, back=1)
                T.matmul(ps_x[:, 0:GROUP], w2[:, :], hid[:, st.slot(4), 0:GROUP], start=True, stop=False)
                for q in range(3):
                    mm = T.matmul(ps_x[:, 0:GROUP], part[:, st.slot(2), q, :], onehot[:, st.slot(2), :], start=False, stop=(q == 2))
                mm.then_inc(S["ext"], 1)

            def turn_results(st):
                after(pe, "x1", st, back=1)
                pe.sem_inc(S["go"], 1)
                with pe.If(general > 0):
                    T.matmul(ps_o[:, 0:GROUP], ones_b[:, :], onehot[:, st.slot(2), :], start=True, stop=True).then_inc(S["seen"], 1)
                    after(pe, "t1", st)
                    after(pe, "cont", st)
                    for q in range(3):
                        mm = T.transpose(ps_o[:, q * P:(q + 1) * P], kept[:, st.slot(2), q * P:(q + 1) * P], ident_f[:, :])
                    mm.then_inc(S["O"], 1)
                with pe.Else():
                    after(pe, "res", st)
                    for q in range(3):
                        mm = T.transpose(ps_o[:, q * P:(q + 1) * P], resT[:, st.slot(2), q * P:(q + 1) * P], ident_f[:, :])
                    mm.then_inc(S["O"], 1)

            loop(pe, turns, [(9, turn_rows), (10, messages), (12, spread), (4, sort), (9, mlp), (10, turn_gains), (12, turn_results), (3, keys)])

        @block.vector
        def _(v):
            V = nc.vector
            done = [0]

            def link(ins):
                done[0] += 1
                ins.then_inc(S["prep"], 1)
                v.wait_ge(S["prep"], done[0])

            v.wait_ge(S["weights"], 7 * 16)
            v.wait_ge(S["const"], 8)
            link(V.tensor_scalar(no_own[:, :], looped[:, :], -1.0, BIG, ALU.add, ALU.mult))
            link(V.tensor_scalar(gap[:, :], no_own[:, :], -1.0, None, ALU.mult))
            link(V.tensor_tensor(b1_own[:, :], b1[:, :], looped[:, :], ALU.mult))
            link(V.tensor_tensor(w1d[:, :], w1a[:, :], w1b[:, :], ALU.subtract))
            link(V.tensor_copy(looped_i[:, :], looped[:, :]))
            link(V.tensor_copy(rounds_f[:, :], rounds_i[:, :]))
            link(V.tensor_scalar(rounds_f[:, :], rounds_f[:, :], 1.5, None, ALU.is_gt))
            link(V.tensor_scalar(general_f[:, :], looped[:, :], 0.0, rounds_f[:, :], ALU.is_equal, ALU.max))
            link(V.tensor_copy(general_i[:, :], general_f[:, :]))
            turns = turns_of(v)
            general = v.value_load(general_i[0:1, 0:1], min_val=0, max_val=1)
            has_loops = v.value_load(looped_i[0:1, 0:1], min_val=0, max_val=1)

            def repeat_places(st):
                landed(v, d_ent, st)
                after(v, "sorted", st, back=2)
                V.tensor_scalar(rep[:, st.slot(2), :], ones_h[:, :], ent[:, st.slot(UN), 2:3], None, ALU.mult).then_inc(S["rep"], 1)

            def rank_edges(st):
                s2 = st.slot(2)
                after(v, "key", st)
                after(v, "pe", st, back=2)
                V.tensor_scalar(junk[:, s2, :], ps_k[:, 0:P], ent[:, st.slot(UN), 2:3], 0.0, ALU.is_lt, ALU.add,
                                accum_out=rank[:, s2:s2 + 1]).then_inc(S["rank"], 1)

            def lanes(st):
                s2 = st.slot(2)
                after(v, "rank", st)
                after(v, "sorted", st, back=2)
                V.tensor_scalar(place[:, s2, :], iota_n[:, :], rank[:, s2:s2 + 1], None, ALU.is_equal).then_inc(S["pe"], 1)

            def lane_changes(st):
                after(v, "pe", st)
                V.tensor_tensor(dplace[:, st.slot(2), :], place[:, st.slot(2), 1:P + 2], place[:, st.slot(2), 0:P + 1],
                                ALU.subtract).then_inc(S["dp"], 1)

            def sorted_edges(st):
                after(v, "sorted", st)
                after(v, "idx", st, per=3, back=2)
                V.tensor_copy(sorted4[:, st.slot(2), :], ps_k[:, 256:260]).then_inc(S["srt"], 1)
                after(v, "scan", st, back=UN)
                V.tensor_scalar(reset[:, st.slot(UN), :], ps_k[:, P:2 * P], 0.0, -BIG, ALU.is_gt, ALU.mult).then_inc(S["srt"], 1)

            def row_numbers(st):
                s2 = st.slot(2)
                after(v, "srt", st, per=2)
                landed(v, d_gat, st, back=4, per=32)
                V.scalar_tensor_tensor(out=idx[:, st.slot(4), 0:1], in0=sorted4[:, s2, 0:1], scalar=256.0, in1=sorted4[:, s2, 1:2],
                                       op0=ALU.mult, op1=ALU.add).then_inc(S["idx"], 1)
                V.tensor_scalar(idx[:, st.slot(4), 1:2], sorted4[:, s2, 2:3], step_f[:, 0, bass.ds(st.t, 1)], float(NPAD - 1),
                                ALU.add, ALU.min).then_inc(S["idx"], 1)
                after(v, "oh", st, back=UN)
                V.scalar_tensor_tensor(out=last_loc[:, st.slot(UN), :], in0=sorted4[:, s2, 3:4], scalar=0.0, in1=sorted4[:, s2, 2:3],
                                       op0=ALU.not_equal, op1=ALU.mult).then_inc(S["idx"], 1)

            def statistics(st):
                s2 = st.slot(2)
                landed(v, d_x, st)
                landed(v, d_gat, st, per=32)
                after(v, "mv", st, per=5, back=2)
                for q in range(5):
                    rows = x3[:, st.slot(UN), q, :] if q < 3 else xg[:, st.slot(4), q - 3, :]
                    V.bn_stats(stats[:, s2, q, :], rows).then_inc(S["bn"], 1)

            def averages(st):
                after(v, "bn", st, per=5)
                after(v, "std", st, back=2)
                v.sem_inc(S["go"], 1)
                for q in range(5):
                    V.bn_aggr(mv[:, st.slot(2), q, :], stats[:, st.slot(2), q, :]).then_inc(S["mv"], 1)

            def scales(st):
                after(v, "std", st)
                after(v, "h", st, per=5, back=4)
                V.reciprocal(rs[:, st.slot(4), :], std[:, st.slot(2), :]).then_inc(S["rs"], 1)

            def shifts(st):
                v.wait_ge(S["rs"], st.count(2) - 1)
                V.scalar_tensor_tensor(out=nm[:, st.slot(4), :], in0=mv[:, st.slot(2), :, 0], scalar=-1.0, in1=rs[:, st.slot(4), :],
                                       op0=ALU.mult, op1=ALU.mult).then_inc(S["rs"], 1)

            def run_maximum(st):
                after(v, "msge", st)
                after(v, "most", st, back=2)
                V.tensor_tensor_scan(out=runmax[:, st.slot(2), :], data0=reset[:, st.slot(UN), :], data1=ps_m[:, P:2 * P],
                                     initial=0.0, op0=ALU.add, op1=ALU.max).then_inc(S["scan"], 1)

            def with_own(st):
                after(v, "scan", st)
                after(v, "gain", st, back=2)
                V.scalar_tensor_tensor(out=reached[:, st.slot(2), :], in0=ps_m[:, 0:P], scalar=no_own[:, :], in1=runmax[:, st.slot(2), :],
                                       op0=ALU.add, op1=ALU.max).then_inc(S["most"], 1)

            def gains(st):
                after(v, "most", st)
                after(v, "scT", st, back=2)
                V.tensor_tensor(gain[:, st.slot(2), :], reached[:, st.slot(2), :], ps_m[:, 0:P], ALU.subtract).then_inc(S["gain"], 1)

            def remainder(st):
                after(v, "hi", st)
                after(v, "lo", st, back=2)
                V.tensor_tensor(rest[:, st.slot(2), :], ps_g[:, 0:P], part[:, st.slot(2), 0, :], ALU.subtract).then_inc(S["r1"], 1)

            def one_hot(st):
                after(v, "ext", st, back=2)
                V.tensor_scalar(onehot[:, st.slot(2), :], iota_loc[:, :, :].rearrange("p t r -> p (t r)"), last_loc[:, st.slot(UN), :],
                                None, ALU.is_equal).then_inc(S["oh"], 1)

            def chunk_maximum(st):
                v.sem_inc(S["go"], 1)
                with v.If(general > 0):
                    after(v, "res", st)
                    after(v, "t1", st)
                    after(v, "carry", st, back=1)
                    V.tensor_copy(carry[:, :], step_f[:, 2, bass.ds(st.t, 1)]).then_inc(S["carry"], 1)
                    after(v, "cont", st, back=1)
                    V.tensor_tensor(found[:, :], resT[:, st.slot(2), :], absent[:, :], ALU.add).then_inc(S["t2"], 1)
                    after(v, "t2", st)
                    after(v, "carry", st)
                    after(v, "O", st, back=2)
                    V.scalar_tensor_tensor(out=kept[:, st.slot(2), :], in0=kept[:, st.slot(2, 1), :], scalar=carry[:, :],
                                           in1=found[:, :], op0=ALU.add, op1=ALU.max).then_inc(S["cont"], 1)

            def add_x(st):
                x_rows = x3[:, st.slot(UN), :, :].rearrange("p t d -> p (t d)")
                after(v, "O", st)
                landed(v, d_x1, st, back=4)
                after(v, "h1", st, per=3, back=4)
                v.sem_inc(S["go"], 1)
                with v.If(has_loops > 0):
                    V.tensor_tensor(x1s[:, st.slot(4), :], x_rows, ps_o[:, 0:GROUP], ALU.add).then_inc(S["x1"], 1)
                with v.Else():
                    after(v, "x1", st, back=1)
                    V.tensor_scalar(raw[:, 0, :], ps_o[:, 0:GROUP], -BIG / 2, None, ALU.is_gt).then_inc(S["raw"], 1)
                    v.wait_ge(S["raw"], st.count(2) - 1)
                    V.tensor_tensor(raw[:, 1, :], ps_o[:, 0:GROUP], raw[:, 0, :], ALU.mult).then_inc(S["raw"], 1)
                    v.wait_ge(S["raw"], st.count(2))
                    V.tensor_tensor(x1s[:, st.slot(4), :], x_rows, raw[:, 1, :], ALU.add).then_inc(S["x1"], 1)

            def statistics1(st):
                after(v, "x1", st)
                after(v, "mv1", st, per=3, back=2)
                for q in range(3):
                    V.bn_stats(stats1[:, st.slot(2), q, :], x1s[:, st.slot(4), q * D:(q + 1) * D]).then_inc(S["bn1"], 1)

            def averages1(st):
                after(v, "bn1", st, per=3)
                after(v, "std1", st, back=2)
                v.sem_inc(S["go"], 1)
                for q in range(3):
                    V.bn_aggr(mv1[:, st.slot(2), q, :], stats1[:, st.slot(2), q, :]).then_inc(S["mv1"], 1)

            def scales1(st):
                after(v, "std1", st)
                after(v, "h1", st, per=3, back=2)
                V.reciprocal(rs1[:, st.slot(2), :], std1[:, st.slot(2), :]).then_inc(S["rs1"], 1)

            def shifts1(st):
                v.wait_ge(S["rs1"], st.count(2) - 1)
                V.scalar_tensor_tensor(out=nm1[:, st.slot(2), :], in0=mv1[:, st.slot(2), :, 0], scalar=-1.0, in1=rs1[:, st.slot(2), :],
                                       op0=ALU.mult, op1=ALU.mult).then_inc(S["rs1"], 1)

            loop(v, turns, [(13, add_x), (11, remainder), (8, scales), (13, statistics1), (8, shifts), (14, scales1), (13, averages1),
                            (14, shifts1), (10, run_maximum), (4, sorted_edges), (10, with_own), (11, one_hot), (10, gains), (12, chunk_maximum), (3, rank_edges),
                            (5, row_numbers), (3, lanes), (2, repeat_places), (7, statistics), (3, lane_changes), (7, averages)])


def layer_gru(nc, env):
    G, TMAX, weights, lists, out = (env[k] for k in ("G", "TMAX", "weights", "lists", "out"))
    x1_dram, h1_dram, step_dram, stepf_dram = (env[k] for k in ("x1_dram", "h1_dram", "step_dram", "stepf_dram"))
    ones_b, ident_f, n_turns, looped, rounds_i = (env[k] for k in ("ones_b", "ident_f", "n_turns", "looped", "rounds_i"))
    NPAD = (G + 1) * GROUP
    H3 = 3 * D
    max_turns = TMAX // UN - PEEL

    with ExitStack() as ctx:
        def sb(name, shape, dt=F32):
            return ctx.enter_context(nc.sbuf_tensor("g_" + name, shape, dt))

        def ps(name):
            return ctx.enter_context(nc.psum_tensor("gp_" + name, [P, 512], F32))

        w_in = sb("w_in", [P, D])
        w_out = sb("w_out", [P, D])
        w_ih = sb("w_ih", [P, 3, 2 * D])
        w_hh = sb("w_hh", [P, 3, D])
        w_ihT = sb("w_ihT", [P, 2, H3])
        lhs = sb("lhs", [P, 3, H3])
        b_side = sb("b_side", [P, 2])
        b_ih = sb("b_ih", [P, 3])
        b_hh = sb("b_hh", [P, 3])
        b_gate = sb("b_gate", [P, 4])
        c_gate = sb("c_gate", [P, 2, 3])
        c_sum = sb("c_sum", [P, 3])
        c_pick = sb("c_pick", [P, 2, TILES, 2 * TILES])
        c_rows = sb("c_rows", [2 * TILES, TILES, H3])
        step_row = sb("step_row", [1, 2, TMAX], I32)
        step_f = sb("step_f", [P, 3, TMAX])
        own_part = sb("own_part", [P, TMAX])
        looped_i = sb("looped_i", [P, 1], I32)
        iota_loc = sb("iota_loc", [P, TILES, P])

        ent = sb("ent", [P, UN, 2, 4], F16)
        idx = sb("idx", [P, 4, 2], I32)
        rows = sb("rows", [P, 4, 2, D])
        part = sb("part", [P, 4, 2, 2, D], F16)
        onehot = sb("onehot", [P, 2, 2, GROUP], F16)
        ones_h = sb("ones_h", [P, 1], F16)
        h_rows = sb("h_rows", [P, 4, TILES * D])
        x_rows = sb("x_rows", [P, 4, TILES * D])
        hT = sb("hT", [P, UN, GROUP])
        sums = sb("sums", [P, 2, 2, GROUP])
        fresh = sb("fresh", [P, 2, GROUP])
        edges = sb("edges", [P, 2, 2, TILES])
        count = sb("count", [P, 2, 2, TILES])
        share = sb("share", [P, 2, 2, TILES])
        mean = sb("mean", [P, 2, 2 * GROUP + P])
        mT0 = sb("mT0", [P, 2, GROUP])
        mT1 = sb("mT1", [P, 2, GROUP + P])
        r = sb("r", [P, 2, GROUP])
        z = sb("z", [P, 4, GROUP])
        rh = sb("rh", [P, 2, GROUP])
        pre = sb("pre", [P, 2, GROUP])
        n = sb("n", [P, 4, GROUP])
        d = sb("d", [P, 2, GROUP])
        e = sb("e", [P, 2, GROUP])
        f = sb("f", [P, 2, GROUP])
        out_rows = sb("out_rows", [P, 4, GROUP])

        ps_s0, ps_s1, ps_r, ps_z, ps_nh, ps_ni, ps_t, ps_o = (ps(q) for q in ("s0", "s1", "r", "z", "nh", "ni", "t", "o"))
        ps_s = (ps_s0, ps_s1)

        names = ("weights const prep turned wcopy idx high low oh agg edges sum fresh count share mean tn tm0 tm1 hT mT0 mT1 "
                 "rg zg nhg nig r z rh pre n d e f to out go").split()
        S = {q: env["ctx"].enter_context(nc.semaphore(f"g_{q}")) for q in names}
        d_ent, d_gat, d_h, d_x, d_out = ([env["ctx"].enter_context(nc.semaphore(f"g_{q}{k}")) for k in range(depth)]
                                         for q, depth in (("ent_in", 4), ("gathered", 4), ("h_in", 4), ("x_in", 4), ("rows_out", 2)))
        block = ctx.enter_context(nc.Block())
        N_LOADS = 6 + 6 + 2

        def turns_of(eng):
            return eng.value_load(n_turns[0:1, 0:1], min_val=1, max_val=max_turns)

        def after(eng, name, st, per=1, back=0):
            if st.past(back):
                eng.wait_ge(S[name], st.count(per, back))

        def landed(eng, sems, st, back=0, per=16):
            if st.past(back):
                eng.wait_ge(sems[st.slot(len(sems), back)], st.landed(len(sems), back, per))

        @block.sync
        def _(sp):
            def load(tile, src):
                sp.dma_start(tile, src).then_inc(S["weights"], 16)

            load(w_in[:, :], weights["W_in"])
            load(w_out[:, :], weights["W_out"])
            load(w_ih[:, :, :], weights["w_ih"].rearrange("(g p) j -> p g j", p=P))
            load(w_hh[:, :, :], weights["w_hh"].rearrange("(g p) j -> p g j", p=P))
            load(b_side[:, 0:1], weights["b_in"].rearrange("(p o) -> p o", o=1))
            load(b_side[:, 1:2], weights["b_out"].rearrange("(p o) -> p o", o=1))
            for tile, name in ((b_ih, "b_ih"), (b_hh, "b_hh")):
                for g in range(3):
                    load(tile[:, g:g + 1], weights[name][g * D:(g + 1) * D].rearrange("(p o) -> p o", o=1))
            load(step_row[:, :, :], step_dram[0:2, :].rearrange("(o k) t -> o k t", o=1))
            load(step_f[:, :, :], stepf_dram.rearrange("(o k) t -> o k t", o=1).broadcast_to([P, 3, TMAX]))
            sp.wait_ge(S["weights"], N_LOADS * 16)
            turns = turns_of(sp)

            def base_of(st):
                return sp.value_load(step_row[0:1, 0, bass.ds(st.t, 1)], min_val=0, max_val=NPAD - GROUP)

            def group_rows(dram, base):
                return dram[bass.ds(base, GROUP), :].rearrange("(p t) d -> p (t d)", t=TILES)

            def entries_in(st):
                chunk = sp.value_load(step_row[0:1, 1, bass.ds(st.t, 1)], min_val=0, max_val=env["CHUNKS"])
                after(sp, "idx", st, back=4)
                sp.sem_inc(S["go"], 1)
                after(sp, "oh", st, per=2, back=UN)
                after(sp, "idx", st, back=4)
                for k in range(2):
                    sp.dma_start(ent[:, st.slot(UN), k, :], lists[k][bass.ds(chunk * P, P), :]).then_inc(d_ent[st.slot(4)], 16)

            def h_in(st):
                base = base_of(st)
                after(sp, "tn", st, back=4)
                sp.sem_inc(S["go"], 1)
                after(sp, "sum", st, per=2, back=4)
                sp.dma_start(h_rows[:, st.slot(4), :], group_rows(h1_dram, base)).then_inc(d_h[st.slot(4)], 16)

            def x_in(st):
                base = base_of(st)
                after(sp, "out", st, back=4)
                sp.dma_start(x_rows[:, st.slot(4), :], group_rows(x1_dram, base)).then_inc(d_x[st.slot(4)], 16)

            def rows_out(st):
                base = base_of(st)
                after(sp, "out", st)
                landed(sp, d_out, st, back=1)
                sp.dma_start(group_rows(out, base), out_rows[:, st.slot(4), :]).then_inc(d_out[st.slot(2)], 16)

            loop(sp, turns, [(0, entries_in), (5, h_in), (11, x_in), (15, rows_out)])
            landed(sp, d_out, Step(turns, PEEL * UN - 1))
            sp.sem_inc(S["go"], 1)

        @block.gpsimd
        def _(pool):
            G_ = nc.gpsimd
            G_.iota(iota_loc[:, :, :], pattern=[[1, TILES], [TILES, P]], base=1, channel_multiplier=0,
                    allow_small_or_imprecise_dtypes=True).then_inc(S["const"], 1)
            G_.memset(ones_h[:, :], 1.0).then_inc(S["const"], 1)
            pool.wait_ge(S["prep"], 12 + 2 * TILES)
            turns = turns_of(pool)

            def gather(st):
                after(pool, "idx", st)
                after(pool, "high", st, back=4)
                after(pool, "low", st, back=4)
                pool.sem_inc(S["go"], 1)
                for k in range(2):
                    G_.indirect_dma_start(out=rows[:, st.slot(4), k, :], out_offset=None, in_=h1_dram[:, :],
                                          in_offset=bass.IndirectOffsetOnAxis(ap=idx[:, st.slot(4), k:k + 1], axis=0)
                                          ).then_inc(d_gat[st.slot(4)], 16)

            def low_part(st):
                after(pool, "high", st)
                after(pool, "agg", st, back=4)
                G_.tensor_tensor(part[:, st.slot(4), 1, :, :], rows[:, st.slot(4), :, :], part[:, st.slot(4), 0, :, :],
                                 ALU.subtract).then_inc(S["low"], 1)

            def blend(st):
                s2 = st.slot(2)
                after(pool, "n", st)
                after(pool, "e", st, back=2)
                G_.tensor_tensor(d[:, s2, :], hT[:, st.slot(UN), :], n[:, st.slot(4), :], ALU.subtract).then_inc(S["d"], 1)
                after(pool, "d", st)
                after(pool, "z", st)
                after(pool, "f", st, back=2)
                G_.tensor_tensor(e[:, s2, :], z[:, st.slot(4), :], d[:, s2, :], ALU.mult).then_inc(S["e"], 1)

            loop(pool, turns, [(12, blend), (6, low_part), (3, gather)])

        @block.scalar
        def _(act):
            A = nc.scalar
            act.wait_ge(S["prep"], 12 + 2 * TILES)
            turns = turns_of(act)

            def high_part(st):
                landed(act, d_gat, st, per=32)
                after(act, "agg", st, back=4)
                A.copy(part[:, st.slot(4), 0, :, :], rows[:, st.slot(4), :, :]).then_inc(S["high"], 1)

            def mean_columns(k):
                def stage(st):
                    after(act, f"tm{k}", st)
                    after(act, "nig", st, back=2)
                    tile = (mT0, mT1)[k]
                    A.copy(tile[:, st.slot(2), :], ps_t[:, 0:tile.shape[2]]).then_inc(S[f"mT{k}"], 1)
                return stage

            def reset_gate(st):
                after(act, "rg", st)
                after(act, "rh", st, back=2)
                A.activation(r[:, st.slot(2), :], ps_r[:, 0:GROUP], ACT.Sigmoid, bias=b_gate[:, 0:1]).then_inc(S["r"], 1)

            def update_gate(st):
                after(act, "zg", st)
                after(act, "e", st, back=4)
                A.activation(z[:, st.slot(4), :], ps_z[:, 0:GROUP], ACT.Sigmoid, bias=b_gate[:, 1:2]).then_inc(S["z"], 1)

            def candidate(st):
                after(act, "pre", st)
                after(act, "f", st, back=4)
                after(act, "d", st, back=4)
                A.activation(n[:, st.slot(4), :], pre[:, st.slot(2), :], ACT.Tanh, bias=b_gate[:, 2:3]).then_inc(S["n"], 1)

            def columns(st):
                after(act, "tn", st)
                after(act, "d", st, back=UN)
                A.copy(hT[:, st.slot(UN), :], ps_t[:, 0:GROUP]).then_inc(S["hT"], 1)

            loop(act, turns, [(8, columns), (8, mean_columns(0)), (11, candidate), (8, mean_columns(1)), (9, reset_gate), (9, update_gate), (5, high_part)])

        @block.tensor
        def _(pe):
            T = nc.tensor
            pe.wait_ge(S["weights"], N_LOADS * 16)
            for g in range(3):
                for side in range(2):
                    T.transpose((ps_r, ps_z)[side][:, g * D:(g + 1) * D], w_ih[:, g, side * D:(side + 1) * D], ident_f[:, :])
                mm = T.transpose(ps_nh[:, g * D:(g + 1) * D], w_hh[:, g, :], ident_f[:, :])
            mm.then_inc(S["turned"], 1)
            pe.wait_ge(S["wcopy"], 3)
            T.matmul(ps_s0[:, 0:H3], w_in[:, :], w_ihT[:, 0, :], start=True, stop=True)
            T.matmul(ps_s1[:, 0:H3], w_out[:, :], w_ihT[:, 1, :], start=True, stop=True)
            pe.wait_ge(S["prep"], 2 + 2 * TILES)
            for t, bank in enumerate((ps_ni, ps_t, ps_r)):
                for side in range(2):
                    T.matmul(bank[0:2 * TILES, 0:H3], c_pick[:, side, t, :], w_ihT[:, side, :], start=(side == 0), stop=(side == 1))
            for side in range(2):
                for g in range(3):
                    mm = T.matmul(ps_o[:, side * 3 + g:side * 3 + g + 1], w_ihT[:, side, g * D:(g + 1) * D], b_side[:, side:side + 1],
                                  start=True, stop=True)
            mm.then_inc(S["turned"], 1)
            pe.wait_ge(S["prep"], 12 + 2 * TILES)
            turns = turns_of(pe)
            has_loops = pe.value_load(looped_i[0:1, 0:1], min_val=0, max_val=1)

            def turn_h(st):
                landed(pe, d_h, st)
                after(pe, "mT1", st, back=1)
                for q in range(TILES):
                    mm = T.transpose(ps_t[:, q * P:(q + 1) * P], h_rows[:, st.slot(4), q * D:(q + 1) * D], ident_f[:, :])
                mm.then_inc(S["tn"], 1)

            def turn_mean(k):
                def stage(st):
                    if k == 0:
                        after(pe, "mean", st)
                        after(pe, "hT", st)
                    else:
                        after(pe, "mT0", st)
                    for q in range(TILES + k):
                        mm = T.transpose(ps_t[:, q * P:(q + 1) * P], mean[:, st.slot(2), (k * TILES + q) * D:(k * TILES + q + 1) * D], ident_f[:, :])
                    mm.then_inc(S[f"tm{k}"], 1)
                return stage

            def aggregate(st):
                after(pe, "low", st)
                after(pe, "oh", st, per=2)
                after(pe, "sum", st, per=2, back=1)
                after(pe, "edges", st, per=2, back=1)
                for k in range(2):
                    for t in range(TILES):
                        chosen = onehot[:, st.slot(2), k, t * P:(t + 1) * P]
                        for q in range(2):
                            T.matmul(ps_s[k][:, t * D:(t + 1) * D], chosen, part[:, st.slot(4), q, k, :], start=(q == 0), stop=(q == 1),
                                     skip_group_check=True)
                        mm = T.matmul(ps_s[k][:, GROUP + t:GROUP + t + 1], chosen, ones_h[:, :], start=True, stop=True, skip_group_check=True)
                mm.then_inc(S["agg"], 1)

            def gates(st):
                s2 = st.slot(2)
                after(pe, "mT1", st)
                after(pe, "hT", st)
                after(pe, "r", st, back=1)
                after(pe, "z", st, back=1)
                after(pe, "pre", st, back=1)
                moving = (mT0[:, s2, :], mT1[:, s2, 0:GROUP], hT[:, st.slot(UN), :])

                def gate(bank, g, sides, name, corrected):
                    for q, side in enumerate(sides):
                        mm = T.matmul(bank[:, 0:GROUP], lhs[:, side, g * D:(g + 1) * D], moving[side], start=(q == 0), stop=(q == len(sides) - 1),
                                      skip_group_check=corrected)
                        if corrected and q == 0:
                            for t in range(TILES):
                                T.matmul(bank[:, t * P:(t + 1) * P], c_rows[:, t, g * D:(g + 1) * D], mT1[0:2 * TILES, s2, GROUP:GROUP + P],
                                         start=False, stop=False, skip_group_check=True)
                    mm.then_inc(S[name], 1)

                pe.sem_inc(S["go"], 1)
                with pe.If(has_loops > 0):
                    gate(ps_r, 0, (0, 1, 2), "rg", False)
                    gate(ps_nh, 2, (2,), "nhg", False)
                    gate(ps_z, 1, (0, 1, 2), "zg", False)
                    gate(ps_ni, 2, (0, 1), "nig", False)
                with pe.Else():
                    gate(ps_r, 0, (0, 1, 2), "rg", True)
                    gate(ps_nh, 2, (2,), "nhg", False)
                    gate(ps_z, 1, (0, 1, 2), "zg", True)
                    gate(ps_ni, 2, (0, 1), "nig", True)

            def turn_out(st):
                after(pe, "f", st)
                after(pe, "out", st, back=1)
                for q in range(3):
                    mm = T.transpose(ps_o[:, q * P:(q + 1) * P], f[:, st.slot(2), q * P:(q + 1) * P], ident_f[:, :])
                mm.then_inc(S["to"], 1)

            loop(pe, turns, [(8, turn_h), (7, aggregate), (8, turn_mean(0)), (14, turn_out), (8, turn_mean(1)), (9, gates)])

        @block.vector
        def _(v):
            V = nc.vector
            done = [0]

            def link(ins):
                done[0] += 1
                ins.then_inc(S["prep"], 1)
                v.wait_ge(S["prep"], done[0])

            v.wait_ge(S["weights"], N_LOADS * 16)
            v.wait_ge(S["const"], 2)
            link(V.memset(c_pick[:, :, :, :], 0.0))
            link(V.memset(mean[:, :, 2 * GROUP:2 * GROUP + P], 0.0))
            for k in range(2):
                for t in range(TILES):
                    link(V.tensor_scalar(c_pick[:, k, t, k * TILES + t:k * TILES + t + 1], b_side[:, k:k + 1], -1.0, None, ALU.mult))
            link(V.memset(edges[:, :, :, :], 0.0))
            link(V.memset(sums[:, :, :, :], 0.0))
            v.wait_ge(S["turned"], 1)
            V.tensor_copy(w_ihT[:, 0, :], ps_r[:, 0:H3]).then_inc(S["wcopy"], 1)
            V.tensor_copy(w_ihT[:, 1, :], ps_z[:, 0:H3]).then_inc(S["wcopy"], 1)
            V.tensor_copy(lhs[:, 2, :], ps_nh[:, 0:H3]).then_inc(S["wcopy"], 1)
            v.wait_ge(S["turned"], 2)
            V.tensor_copy(lhs[:, 0, :], ps_s0[:, 0:H3]).then_inc(S["wcopy"], 1)
            V.tensor_copy(lhs[:, 1, :], ps_s1[:, 0:H3]).then_inc(S["wcopy"], 1)
            for t, bank in enumerate((ps_ni, ps_t, ps_r)):
                V.tensor_copy(c_rows[:, t, :], bank[0:2 * TILES, 0:H3]).then_inc(S["wcopy"], 1)
            v.wait_ge(S["wcopy"], 5 + TILES)
            link(V.tensor_copy(c_gate[:, :, :], ps_o[:, 0:6].rearrange("p (s g) -> p s g", s=2)))
            link(V.tensor_tensor(c_sum[:, :], c_gate[:, 0, :], c_gate[:, 1, :], ALU.add))
            link(V.tensor_tensor(c_sum[:, :], c_sum[:, :], b_ih[:, :], ALU.add))
            link(V.tensor_tensor(b_gate[:, 0:2], c_sum[:, 0:2], b_hh[:, 0:2], ALU.add))
            link(V.tensor_copy(b_gate[:, 2:3], c_sum[:, 2:3]))
            link(V.tensor_copy(b_gate[:, 3:4], b_hh[:, 2:3]))
            link(V.tensor_scalar(own_part[:, :], step_f[:, 1, :], 0.0, looped[:, :], ALU.is_equal, ALU.mult))
            link(V.tensor_copy(looped_i[:, :], looped[:, :]))
            link(V.memset(fresh[:, :, :], 0.0))
            link(V.memset(share[:, :, :, :], 0.0))
            turns = turns_of(v)
            rounds = v.value_load(rounds_i[0:1, 0:1], min_val=1, max_val=env["ROUNDS"])

            def row_numbers(st):
                landed(v, d_ent, st, per=32)
                landed(v, d_gat, st, back=4, per=32)
                V.scalar_tensor_tensor(out=idx[:, st.slot(4), :], in0=ent[:, st.slot(UN), :, 0], scalar=256.0, in1=ent[:, st.slot(UN), :, 1],
                                       op0=ALU.mult, op1=ALU.add).then_inc(S["idx"], 1)

            def one_hots(st):
                after(v, "agg", st, back=2)
                for k in range(2):
                    V.tensor_scalar(onehot[:, st.slot(2), k, :], iota_loc[:, :, :].rearrange("p t r -> p (t r)"), ent[:, st.slot(UN), k, 2:3],
                                    None, ALU.is_equal).then_inc(S["oh"], 1)

            def add_sums(st):
                s2 = st.slot(2)
                after(v, "agg", st)
                after(v, "edges", st, per=2, back=1)
                for k in range(2):
                    V.scalar_tensor_tensor(out=edges[:, s2, k, :], in0=edges[:, 1 - s2, k, :], scalar=step_f[:, 1, bass.ds(st.t, 1)],
                                           in1=ps_s[k][:, GROUP:GROUP + TILES], op0=ALU.mult, op1=ALU.add).then_inc(S["edges"], 1)
                landed(v, d_h, st)
                after(v, "mean", st, back=2)
                v.sem_inc(S["go"], 1)

                def whole(out, scalar, k, name):
                    V.scalar_tensor_tensor(out=out, in0=h_rows[:, st.slot(4), :], scalar=scalar, in1=ps_s[k][:, 0:GROUP],
                                           op0=ALU.mult, op1=ALU.add).then_inc(S[name], 1)

                with v.If(rounds > 1):
                    after(v, "sum", st, per=2, back=1)
                    for k in range(2):
                        whole(fresh[:, k, :], own_part[:, bass.ds(st.t, 1)], k, "fresh")
                    after(v, "fresh", st, per=2)
                    for k in range(2):
                        V.scalar_tensor_tensor(out=sums[:, s2, k, :], in0=sums[:, 1 - s2, k, :], scalar=step_f[:, 1, bass.ds(st.t, 1)],
                                               in1=fresh[:, k, :], op0=ALU.mult, op1=ALU.add).then_inc(S["sum"], 1)
                with v.Else():
                    for k in range(2):
                        whole(sums[:, s2, k, :], looped[:, :], k, "sum")

            def counts(st):
                s2 = st.slot(2)
                after(v, "edges", st, per=2)
                after(v, "tm1", st, back=2)
                V.tensor_scalar(count[:, s2, :, :], edges[:, s2, :, :], looped[:, :], 1.0, ALU.add, ALU.max).then_inc(S["count"], 1)
                V.tensor_scalar(mean[:, s2, 2 * GROUP:2 * GROUP + 2 * TILES], edges[:, s2, :, :].rearrange("p k t -> p (k t)"), 0.5, None,
                                ALU.is_lt).then_inc(S["count"], 1)

            def shares(st):
                after(v, "count", st, per=2)
                V.reciprocal(share[:, st.slot(2), :, :], count[:, st.slot(2), :, :]).then_inc(S["share"], 1)

            def means(st):
                s2 = st.slot(2)
                after(v, "share", st)
                after(v, "sum", st, per=2)
                V.tensor_tensor(mean[:, s2, 0:2 * GROUP].rearrange("p (k d) -> p k d", d=D),
                                sums[:, s2, :, :].rearrange("p k (t d) -> p (k t) d", d=D),
                                share[:, s2, :, :].rearrange("p k t -> p (k t)").unsqueeze(2).to_broadcast([P, 2 * TILES, D]),
                                ALU.mult).then_inc(S["mean"], 1)

            def reset_part(st):
                after(v, "r", st)
                after(v, "nhg", st)
                after(v, "pre", st, back=2)
                V.scalar_tensor_tensor(out=rh[:, st.slot(2), :], in0=ps_nh[:, 0:GROUP], scalar=b_gate[:, 3:4], in1=r[:, st.slot(2), :],
                                       op0=ALU.add, op1=ALU.mult).then_inc(S["rh"], 1)

            def before_tanh(st):
                after(v, "rh", st)
                after(v, "nig", st)
                after(v, "n", st, back=2)
                V.tensor_tensor(pre[:, st.slot(2), :], ps_ni[:, 0:GROUP], rh[:, st.slot(2), :], ALU.add).then_inc(S["pre"], 1)

            def new_h(st):
                after(v, "e", st)
                after(v, "to", st, back=2)
                V.tensor_tensor(f[:, st.slot(2), :], n[:, st.slot(4), :], e[:, st.slot(2), :], ALU.add).then_inc(S["f"], 1)

            def add_x(st):
                landed(v, d_x, st)
                after(v, "to", st)
                landed(v, d_out, st, back=4)
                V.tensor_tensor(out_rows[:, st.slot(4), :], x_rows[:, st.slot(4), :], ps_o[:, 0:GROUP], ALU.add).then_inc(S["out"], 1)

            loop(v, turns, [(10, before_tanh), (7, add_sums), (7, counts), (13, new_h), (7, shares), (2, row_numbers), (6, one_hots), (14, add_x),
                            (7, means), (9, reset_part)])


def layout(x, src, dst):
    import numpy as np
    n, e = x.shape[0], src.shape[0]
    groups, cols, _, _ = sizes(n, e)
    x_pad = np.zeros(((groups + 1) * GROUP, D), x.dtype)
    x_pad[:n] = x
    src_pad = np.zeros(P * cols, src.dtype)
    src_pad[:e] = src
    dst_pad = np.full(P * cols + 1, 2 * n, dst.dtype)
    dst_pad[:e] = dst
    return {"x": x_pad, "src": src_pad, "dst": dst_pad}



def kernel(**inputs):
    import numpy as np
    import concourse.bacc as _bacc
    from concourse import mybir as _mybir
    from concourse.bass_utils import run_bass_kernel_spmd as _run

    x, src, dst = (np.ascontiguousarray(inputs[name]) for name in ("x", "src", "dst"))
    n_nodes, n_edges = x.shape[0], src.shape[0]
    arrays = layout(x, src, dst)
    for layer, names in (("L0_gnn_", ("W1", "b1", "W2", "b2")),
                         ("L1_gnn_", ("W_in", "b_in", "W_out", "b_out", "w_ih", "w_hh", "b_ih", "b_hh"))):
        for name in names:
            arrays[name] = np.ascontiguousarray(inputs[layer + name])

    nc = _bacc.Bacc("TRN2", target_bir_lowering=False, num_devices=1)
    ins = {name: nc.dram_tensor(f"in_{name}_dram", a.shape, _mybir.dt.from_np(a.dtype), kind="ExternalInput").ap()
           for name, a in arrays.items()}
    rows = (sizes(n_nodes, n_edges)[0] + 1) * GROUP
    out = nc.dram_tensor("out_0_dram", (rows, D), _mybir.dt.float32, kind="ExternalOutput").ap()
    build(nc, n_nodes, n_edges, ins["x"], ins["src"], ins["dst"], ins, out)
    r = _run(nc, [{f"in_{name}_dram": a for name, a in arrays.items()}], core_ids=[0])
    return r.results[0]["out_0_dram"][:n_nodes]
```

```python
from contextlib import ExitStack

import concourse.bass as bass
from concourse import mybir

P = 128
D = 128
TILES = 3
GROUP = TILES * P
UN = 8
PEEL = 3
U = 8
BIG = 3.0e38
RESET = 2.0e35
EPS = 1e-5

F32 = mybir.dt.float32
F16 = mybir.dt.float16
BF16 = mybir.dt.bfloat16
I32 = mybir.dt.int32
ALU = mybir.AluOpType
ACT = mybir.ActivationFunctionType
AX = mybir.AxisListType.X
RMAX = bass.bass_isa.ReduceOp.max


def sizes(n_nodes, n_edges):
    groups = -(-n_nodes // GROUP)
    cols = -(-n_edges // (P * 2 * U)) * 2 * U
    rounds = -(-n_edges // P)
    steps = max(2, -(-(groups + 2 * rounds + (PEEL + 1) * UN) // P))
    return groups, cols, rounds, steps


class Step:

    def __init__(self, i, c):
        self.i, self.c = i, c
        self.peeled = isinstance(i, int)

    @property
    def t(self):
        return self.i * UN + self.c

    def past(self, back):
        return not self.peeled or self.t >= back

    def slot(self, depth, back=0):
        return (self.c - back) % depth

    def count(self, per=1, back=0):
        return (self.i * UN + (self.c - back + 1)) * per

    def landed(self, turns, back=0, per=16):
        return (self.i * (UN // turns) + ((self.c - back) // turns + 1)) * per


def loop(eng, turns, stages):
    for n in range(PEEL * UN):
        for lag, stage in stages:
            if n >= lag:
                stage(Step(0, n - lag))
    with eng.Fori(0, turns) as i:
        for n in range(PEEL * UN, (PEEL + 1) * UN):
            for lag, stage in stages:
                stage(Step(i, n - lag))
    for n in range(max(lag for lag, _ in stages)):
        for lag, stage in stages:
            if n < lag:
                stage(Step(turns, PEEL * UN + n - lag))


def build(nc, n_nodes, n_edges, x, src, dst, weights, out):
    G, COLS, ROUNDS, TC = sizes(n_nodes, n_edges)
    CHUNKS = ROUNDS * G
    TMAX = P * TC
    NO_LIST = float(1 << 20)

    lists = [nc.dram_tensor(f"lists_{by}", ((CHUNKS + 1) * P, 4), F16, kind="Internal").ap() for by in ("dst", "src")]
    step_dram = nc.dram_tensor("step_dram", (2, TMAX), I32, kind="Internal").ap()
    stepf_dram = nc.dram_tensor("stepf_dram", (4, TMAX), F32, kind="Internal").ap()

    x1_dram = nc.dram_tensor("x1_dram", ((G + 1) * GROUP, D), F32, kind="Internal").ap()
    h1_dram = nc.dram_tensor("h1_dram", ((G + 1) * GROUP, D), F32, kind="Internal").ap()

    ctx = ExitStack()
    with ctx:
        def sb(name, shape, dt):
            return ctx.enter_context(nc.sbuf_tensor(name, shape, dt))

        def ps(name, shape, dt=F32):
            return ctx.enter_context(nc.psum_tensor(name, shape, dt))

        def sem(name):
            return ctx.enter_context(nc.semaphore(name))

        ones_f = sb("ones_f", [P, P], F32)
        ones_b = sb("ones_b", [P, P], BF16)
        ident_f = sb("ident_f", [P, P], F32)
        before = sb("before", [P, P], BF16)
        not_before = sb("not_before", [P, P], BF16)
        iota_g = sb("iota_g", [P, G], F32)
        iota_c = sb("iota_c", [P, COLS], F32)
        iota_t = sb("iota_t", [P, TC], F32)
        sentinel = sb("sentinel", [P, G, 4], F16)

        looped = sb("looped", [P, 1], F32)
        rounds_i = sb("rounds_i", [P, 1], I32)
        n_turns = sb("n_turns", [P, 1], I32)

        step_row = sb("step_row", [1, 2, TMAX], I32)
        step_f = sb("step_f", [P, 4, TMAX], F32)

        with ExitStack() as prep:
            def tb(name, shape, dt):
                return prep.enter_context(nc.sbuf_tensor(name, shape, dt))
            planes = [tb(f"planes{n}", [P, 3, COLS], I32) for n in range(2)]
            nxt_i = tb("nxt_i", [P, COLS], I32)
            mask = tb("mask", [P, COLS], I32)
            zero_c = tb("zero_c", [P, COLS], I32)
            sf = tb("sf", [P, COLS], F32)
            df = tb("df", [P, COLS], F32)
            nf = tb("nf", [P, COLS], F32)
            flag = tb("flag", [P, COLS], F32)
            viol = tb("viol", [P, COLS], F32)
            cum = tb("cum", [P, COLS], F32)
            ones_c = tb("ones_c", [P, COLS], F32)
            key = tb("key", [P, 2, COLS], F32)
            quot_i = tb("quot_i", [P, 2, COLS], I32)
            quot = tb("quot", [P, 2, COLS], F32)
            loc = tb("loc", [P, 2, COLS], F32)
            over = tb("over", [P, 2, COLS], F32)
            entries = tb("entries", [P, 2, COLS, 4], F16)
            red = tb("red", [P, 8], F32)
            kept = tb("kept", [P, 2], F32)
            kept_i = tb("kept_i", [P, 8], I32)
            B = tb("B", [P, 4, G], BF16)
            prod = tb("prod", [P, 4, G], F32)
            kb8 = tb("kb8", [P, 2, 2, U], F32)
            rk8 = tb("rk8", [P, 2, 2, U], F32)
            ri8 = tb("ri8", [P, 3, 2, U], I32)
            rf8 = tb("rf8", [P, 2, 2, U], F32)
            pos8 = tb("pos8", [P, 2, 2, U], I32)
            ent8 = tb("ent8", [P, 2, 2, U, 4], F16)
            nb_i = tb("nb_i", [P, 2, G], I32)
            nb_f = tb("nb_f", [P, 2, G], F32)
            chunks = tb("chunks", [P, G], F32)
            ends = tb("ends", [P, G], F32)
            hit = tb("hit", [P, G], F32)
            tt = tb("tt", [P, 8, TC], F32)
            tf = tb("tf", [P, 4, TC], F32)
            ti = tb("ti", [P, 2, TC], I32)
            zero_b = tb("zero_b", [P, P], BF16)
            zero_g = tb("zero_g", [P, G], BF16)
            rank_ps = [prep.enter_context(nc.psum_tensor(f"rank_ps{k}", [P, 512], F32)) for k in range(2)]
            sum_ps = prep.enter_context(nc.psum_tensor("sum_ps", [P, 512], F32))

            s_load = sem("edges_loaded")
            s_const = sem("constants_ready")
            s_tmp = sem("pool_constants")
            s_v = sem("prep_vector")
            s_red = sem("partition_sums_ready")
            s_sum = sem("sums_ready")
            s_kept = sem("kept_counts_ready")
            s_kmax = sem("kept_maximum_ready")
            s_loops = sem("rank_trips_ready")
            s_fill = sem("lists_cleared")
            s_go = sem("second_scatter_started")
            s_rmax = sem("rounds_ready")
            s_tab = sem("step_table_ready")
            s_tabw = sem("step_table_moved")
            rank_sems = [dict(zero=sem(f"rank_sums_cleared{q}"), onehot=sem(f"onehot_ready{q}"),
                              rank=sem(f"ranks_summed{q}"), read=sem(f"rank_read{q}"),
                              pos=sem(f"positions_ready{q}"), scat=[sem(f"scattered{q}{h}") for h in range(2)],
                              last=sem(f"rank_sums_final{q}")) for q in range(2)]

            s_chain = [sem("rank_vector0"), sem("rank_vector1")]

            block = prep.enter_context(nc.Block())

            @block.sync
            def _(sp):
                sp.dma_start(planes[0][:, 0, :], src.rearrange("(p c) -> p c", p=P)).then_inc(s_load, 16)
                sp.dma_start(planes[0][:, 1, :], dst[0:P * COLS].rearrange("(p c) -> p c", p=P)).then_inc(s_load, 16)
                sp.dma_start(nxt_i[:, :], dst[1:P * COLS + 1].rearrange("(p c) -> p c", p=P)).then_inc(s_load, 16)
                sp.wait_ge(s_const, 1)
                for k in range(2):
                    sp.dma_start(lists[k][0:G * P, :].rearrange("(p g) e -> p g e", p=P), sentinel[:, :, :]).then_inc(s_fill, 16)
                    sp.dma_start(lists[k][CHUNKS * P:(CHUNKS + 1) * P, :], sentinel[:, 0, :]).then_inc(s_fill, 16)
                sp.wait_ge(s_rmax, 1)
                rmax = sp.value_load(kept_i[0:1, 2:3], min_val=1, max_val=ROUNDS)
                trips = sp.value_load(kept_i[0:1, 1:2], min_val=1, max_val=COLS // (2 * U))
                for h in range(2):
                    sp.wait_ge(rank_sems[0]["scat"][h], trips * (2 * U * 16))
                    sp.sem_inc(s_go, 1)
                with sp.If(rmax > 1):
                    with sp.Fori(1, rmax) as r:
                        for k in range(2):
                            sp.dma_start(lists[k][bass.ds(r * (G * P), G * P), :].rearrange("(p g) e -> p g e", p=P),
                                         sentinel[:, :, :]).then_inc(s_fill, 16)
                    for h in range(2):
                        sp.wait_ge(rank_sems[1]["scat"][h], trips * (2 * U * 16))
                        sp.sem_inc(s_go, 1)
                sp.wait_ge(s_tab, 1)
                sp.dma_start(step_dram.rearrange("k (p c) -> p k c", p=P), ti[:, :, :]).then_inc(s_tabw, 16)
                sp.dma_start(stepf_dram.rearrange("k (p c) -> p k c", p=P), tf[:, :, :]).then_inc(s_tabw, 16)
                sp.wait_ge(s_tabw, 32)
                turns = sp.value_load(n_turns[0:1, 0:1], min_val=1, max_val=TMAX // UN - PEEL)

                def table_in(first, last):
                    sp.dma_start(step_row[:, :, first:last], step_dram[:, first:last].rearrange("(o k) t -> o k t", o=1)).then_inc(s_tabw, 16)
                    sp.dma_start(step_f[:, :, first:last], stepf_dram[:, first:last].rearrange("(o k) t -> o k t", o=1)
                                 .broadcast_to([P, 4, last - first])).then_inc(s_tabw, 16)

                usual = min(TMAX, -(-(G + 1) // UN) * UN * 3 // 2)
                table_in(0, usual)
                sp.wait_ge(s_tabw, 64)
                if usual < TMAX:
                    with sp.If(turns > usual // UN - PEEL):
                        table_in(usual, TMAX)
                        sp.wait_ge(s_tabw, 96)

            @block.gpsimd
            def _(pool):
                nc.gpsimd.memset(sentinel[:, :, :], 0.0).then_inc(s_tmp, 1)
                pool.wait_ge(s_tmp, 1)
                nc.gpsimd.memset(sentinel[:, :, 2], 1000.0).then_inc(s_tmp, 1)
                pool.wait_ge(s_tmp, 2)
                nc.gpsimd.iota(iota_g[:, :], pattern=[[1, G]], base=0, channel_multiplier=0,
                               allow_small_or_imprecise_dtypes=True).then_inc(s_const, 1)
                nc.gpsimd.iota(iota_c[:, :], pattern=[[1, COLS]], base=0, channel_multiplier=0,
                               allow_small_or_imprecise_dtypes=True).then_inc(s_const, 1)
                nc.gpsimd.iota(iota_t[:, :], pattern=[[1, TC]], base=0, channel_multiplier=TC,
                               allow_small_or_imprecise_dtypes=True).then_inc(s_const, 1)
                nc.gpsimd.memset(ones_b[:, :], 1.0).then_inc(s_const, 1)
                nc.gpsimd.memset(ones_f[:, :], 1.0).then_inc(s_const, 1)
                nc.gpsimd.memset(ident_f[:, :], 0.0).then_inc(s_const, 1)
                pool.wait_ge(s_const, 6)
                nc.gpsimd.affine_select(out=ident_f[:, :], in_=ident_f[:, :], compare_op=ALU.not_equal, fill=1.0,
                                        base=0, pattern=[[-1, P]], channel_multiplier=1).then_inc(s_const, 1)
                nc.gpsimd.affine_select(out=before[:, :], in_=ones_b[:, :], compare_op=ALU.is_gt, fill=0.0,
                                        base=0, pattern=[[1, P]], channel_multiplier=-1).then_inc(s_const, 1)
                nc.gpsimd.affine_select(out=not_before[:, :], in_=ones_b[:, :], compare_op=ALU.is_ge, fill=0.0,
                                        base=0, pattern=[[-1, P]], channel_multiplier=1).then_inc(s_const, 1)
                nc.gpsimd.memset(zero_b[:, :], 0.0).then_inc(s_const, 1)
                pool.wait_ge(s_kept, 1)
                nc.gpsimd.partition_all_reduce(kept[:, 1:2], kept[:, 0:1], P, RMAX).then_inc(s_kmax, 1)
                pool.wait_ge(s_loops, 1)
                trips = pool.value_load(kept_i[0:1, 1:2], min_val=1, max_val=COLS // (2 * U))
                pool.wait_ge(s_fill, 64)

                def scatter(sems):
                    with pool.Fori(0, trips) as i:
                        for h in range(2):
                            pool.wait_ge(sems["pos"], 2 * i + h + 1)
                            pool.sem_inc(s_go, 1)
                            for k in range(2):
                                for u in range(U):
                                    nc.gpsimd.indirect_dma_start(
                                        out=lists[k][:, :], out_offset=bass.IndirectOffsetOnAxis(ap=pos8[:, h, k, u:u + 1], axis=0),
                                        in_=ent8[:, h, k, u, :], in_offset=None,
                                        bounds_check=CHUNKS * P - 1, oob_is_err=False).then_inc(sems["scat"][h], 16)

                scatter(rank_sems[0])
                pool.wait_ge(s_rmax, 1)
                rmax = pool.value_load(kept_i[0:1, 2:3], min_val=1, max_val=ROUNDS)
                with pool.If(rmax > 1):
                    pool.wait_ge(s_fill, rmax * 32 + 32)
                    pool.sem_inc(s_go, 1)
                    scatter(rank_sems[1])

            @block.tensor
            def _(pe):
                pe.wait_ge(s_const, 10)
                pe.wait_ge(s_red, 1)
                nc.tensor.matmul(sum_ps[:, 0:2], ones_f[:, :], red[:, 0:2], start=True, stop=True).then_inc(s_sum, 1)
                pe.wait_ge(s_loops, 1)
                trips = pe.value_load(kept_i[0:1, 1:2], min_val=1, max_val=COLS // (2 * U))

                def rank(sems):
                    N = 2 * U * 2
                    for k in range(2):
                        mm = nc.tensor.matmul(rank_ps[k][:, 0:G], zero_b[:, :], zero_g[:, :], start=True, stop=False, skip_group_check=True)

                    def first(n, i):
                        pe.wait_ge(sems["onehot"], i * N + n + 1)
                        nc.tensor.matmul(rank_ps[n % 2][:, 0:G], before[:, :], B[:, n % 4, :],
                                         start=False, stop=False, skip_group_check=True).then_inc(sems["rank"], 1)

                    def second(n, i):
                        pe.wait_ge(sems["read"], i * N + n + 1)
                        mm = nc.tensor.matmul(rank_ps[n % 2][:, 0:G], not_before[:, :], B[:, n % 4, :],
                                         start=False, stop=False, skip_group_check=True)
                        mm.then_inc(sems["last"], 1)

                    with pe.Fori(0, trips) as i:
                        first(0, i)
                        for n in range(1, N):
                            first(n, i)
                            second(n - 1, i)
                        second(N - 1, i)

                pe.wait_ge(rank_sems[0]["zero"], 1)
                rank(rank_sems[0])
                pe.wait_ge(s_rmax, 1)
                rmax = pe.value_load(kept_i[0:1, 2:3], min_val=1, max_val=ROUNDS)
                with pe.If(rmax > 1):
                    pe.wait_ge(rank_sems[1]["zero"], 1)
                    rank(rank_sems[1])

            @block.vector
            def _(v):
                done = [0]

                def sent(ins):
                    done[0] += 1
                    ins.then_inc(s_v, 1)

                def link(ins):
                    sent(ins)
                    v.wait_ge(s_v, done[0])

                V = nc.vector
                link(V.memset(ones_c[:, :], 1.0))
                link(V.memset(zero_c[:, :], 0))
                link(V.memset(entries[:, :, :, 3], 0.0))
                link(V.memset(zero_g[:, :], 0.0))
                v.wait_ge(s_load, 48)
                cur = planes[0]
                link(V.tensor_copy(sf[:, :], cur[:, 0, :]))
                link(V.tensor_copy(df[:, :], cur[:, 1, :]))
                link(V.tensor_copy(nf[:, :], nxt_i[:, :]))
                link(V.tensor_tensor(flag[:, :], sf[:, :], df[:, :], ALU.is_equal))
                link(V.tensor_tensor(viol[:, :], nf[:, :], df[:, :], ALU.not_equal))
                link(V.tensor_tensor(flag[:, :], flag[:, :], viol[:, :], ALU.mult))
                link(V.tensor_tensor(viol[:, :], nf[:, :], df[:, :], ALU.is_lt))
                link(V.tensor_reduce(red[:, 0:1], flag[:, :], AX, ALU.add))
                V.tensor_reduce(red[:, 1:2], viol[:, :], AX, ALU.add).then_inc(s_red, 1)
                v.wait_ge(s_sum, 1)
                link(V.tensor_scalar(red[:, 2:3], sum_ps[:, 0:1], float(n_nodes), None, ALU.is_equal))
                link(V.tensor_scalar(red[:, 3:4], sum_ps[:, 1:2], 0.0, None, ALU.is_equal))
                link(V.tensor_tensor(looped[:, :], red[:, 2:3], red[:, 3:4], ALU.mult))
                link(V.tensor_scalar(viol[:, :], df[:, :], 1.5 * n_nodes, None, ALU.is_lt))
                link(V.scalar_tensor_tensor(out=nf[:, :], in0=flag[:, :], scalar=looped[:, 0:1], in1=viol[:, :], op0=ALU.mult, op1=ALU.subtract))
                link(V.tensor_scalar(flag[:, :], nf[:, :], 1.0, None, ALU.add))
                link(V.tensor_tensor_scan(out=cum[:, :], data0=ones_c[:, :], data1=flag[:, :], initial=0.0, op0=ALU.mult, op1=ALU.add))
                link(V.scalar_tensor_tensor(out=cur[:, 2, :], in0=cum[:, :], scalar=-1.0, in1=nf[:, :], op0=ALU.mult, op1=ALU.mult))
                V.tensor_scalar(kept[:, 0:1], cum[:, COLS - 1:COLS], -1.0, float(COLS), ALU.mult, ALU.add).then_inc(s_kept, 1)
                bit = 1
                while bit < COLS:
                    new = planes[1] if cur is planes[0] else planes[0]
                    sent(V.tensor_scalar(mask[:, :], cur[:, 2, :], bit, None, ALU.bitwise_and))
                    link(V.tensor_copy(new[:, :, :], cur[:, :, :]))
                    sent(V.copy_predicated(new[:, 2, :], mask[:, :], zero_c[:, :]))
                    for q in (0, 1, 2):
                        if q == 2:
                            v.wait_ge(s_v, done[0] - 2)
                        sent(V.copy_predicated(new[:, q, 0:COLS - bit], mask[:, bit:COLS], cur[:, q, bit:COLS]))
                    v.wait_ge(s_v, done[0])
                    cur, bit = new, bit * 2
                v.wait_ge(s_kmax, 1)
                link(V.tensor_scalar(kept_i[:, 0:1], kept[:, 1:2], float(2 * U - 1), None, ALU.add))
                link(V.tensor_scalar(kept_i[:, 3:4], kept_i[:, 0:1], (2 * U).bit_length() - 1, None, ALU.arith_shift_right))
                V.tensor_scalar(kept_i[:, 1:2], kept_i[:, 3:4], 1.0, None, ALU.max).then_inc(s_loops, 1)
                link(V.tensor_copy(key[:, 0, :], cur[:, 1, :]))
                link(V.tensor_copy(key[:, 1, :], cur[:, 0, :]))
                link(V.tensor_scalar(quot_i[:, :, :], key[:, :, :], 1.0 / GROUP, 0.5 / GROUP, ALU.mult, ALU.add))
                link(V.tensor_copy(quot[:, :, :], quot_i[:, :, :]))
                link(V.scalar_tensor_tensor(out=loc[:, :, :], in0=quot[:, :, :], scalar=-float(GROUP), in1=key[:, :, :], op0=ALU.mult, op1=ALU.add))
                link(V.tensor_scalar(over[:, :, :], loc[:, :, :], 0.0, None, ALU.is_lt))
                link(V.scalar_tensor_tensor(out=loc[:, :, :], in0=over[:, :, :], scalar=float(GROUP), in1=loc[:, :, :], op0=ALU.mult, op1=ALU.add))
                link(V.tensor_tensor(quot[:, :, :], quot[:, :, :], over[:, :, :], ALU.subtract))
                link(V.tensor_scalar(over[:, 0, :], iota_c[:, :], kept[:, 0:1], NO_LIST, ALU.is_ge, ALU.mult))
                for k in range(2):
                    link(V.tensor_tensor(quot[:, k, :], quot[:, k, :], over[:, 0, :], ALU.add))
                    link(V.tensor_scalar(mask[:, :], cur[:, k, :], 8, None, ALU.arith_shift_right))
                    link(V.tensor_copy(entries[:, k, :, 0], mask[:, :]))
                    link(V.tensor_scalar(nxt_i[:, :], cur[:, k, :], 255, None, ALU.bitwise_and))
                    link(V.tensor_copy(entries[:, k, :, 1], nxt_i[:, :]))
                    link(V.tensor_scalar(entries[:, k, :, 2], loc[:, k, :], 1.0, None, ALU.add))
                trips = v.value_load(kept_i[0:1, 1:2], min_val=1, max_val=COLS // (2 * U))
                v.wait_ge(s_const, 10)

                def rank(sems, chain):
                    N = 2 * U * 2
                    PER = 9

                    def onehot(n, i):
                        h, u, k = n // (2 * U), n // 2 % U, n % 2
                        if n >= 4:
                            v.wait_ge(sems["last"], i * N + n - 3)
                        V.tensor_scalar(B[:, n % 4, :], iota_g[:, :], kb8[:, h, k, u:u + 1], None, ALU.is_equal).then_inc(sems["onehot"], 1)

                    def read(n, i):
                        h, u, k = n // (2 * U), n // 2 % U, n % 2
                        v.wait_ge(sems["rank"], i * N + n + 1)
                        V.tensor_tensor_reduce(prod[:, n % 4, :], B[:, n % 4, :], rank_ps[k][:, 0:G], 1.0, 0.0, ALU.mult, ALU.add,
                                               rk8[:, h, k, u:u + 1]).then_inc(sems["read"], 1)

                    with v.Fori(0, trips) as i:
                        def columns(h):
                            v.wait_ge(sems["scat"][h], i * (2 * U * 16))
                            c0 = i * (2 * U) + h * U
                            V.tensor_copy(kb8[:, h, :, :], quot[:, :, bass.ds(c0, U)]).then_inc(chain, 1)
                            V.tensor_copy(ent8[:, h, :, :, :], entries[:, :, bass.ds(c0, U), :]).then_inc(chain, 1)

                        columns(0)
                        v.wait_ge(chain, i * (2 * PER) + 2)
                        v.wait_ge(sems["last"], i * N)
                        for n in range(2):
                            onehot(n, i)
                        for n in range(N):
                            read(n, i)
                            if n % (2 * U) < 2 * U - 2:
                                onehot(n + 2, i)
                            if n % (2 * U) == 2 * U - 1:
                                h = n // (2 * U)
                                at = [2 + PER * h]

                                def step(ins):
                                    at[0] += 1
                                    ins.then_inc(chain, 1)
                                    v.wait_ge(chain, i * (2 * PER) + at[0])

                                v.wait_ge(sems["read"], i * N + n + 1)
                                step(V.tensor_copy(ri8[:, 0], rk8[:, h]))
                                step(V.tensor_scalar(ri8[:, 1], ri8[:, 0], 7, None, ALU.arith_shift_right))
                                step(V.tensor_scalar(ri8[:, 2], ri8[:, 0], P - 1, None, ALU.bitwise_and))
                                step(V.tensor_copy(rf8[:, 0], ri8[:, 1]))
                                step(V.scalar_tensor_tensor(out=ri8[:, 0], in0=rf8[:, 0], scalar=float(G), in1=kb8[:, h], op0=ALU.mult, op1=ALU.add))
                                step(V.tensor_scalar(ri8[:, 1], ri8[:, 0], 7, None, ALU.logical_shift_left))
                                step(V.tensor_tensor(pos8[:, h], ri8[:, 1], ri8[:, 2], ALU.bitwise_or))
                                V.tensor_copy(rf8[:, 1], rf8[:, 0]).then_inc(sems["pos"], 1)
                                if h == 0:
                                    columns(1)
                                    v.wait_ge(chain, i * (2 * PER) + PER + 2)
                                    onehot(2 * U, i)
                                    onehot(2 * U + 1, i)

                def counts():
                    link(V.tensor_copy(nb_f[:, 0, :], rank_ps[0][:, 0:G]))
                    link(V.tensor_copy(nb_f[:, 1, :], rank_ps[1][:, 0:G]))
                    link(V.tensor_scalar(nb_i[:, :, :], nb_f[:, :, :], float(P - 1), None, ALU.add))
                    link(V.tensor_scalar(nb_i[:, :, :], nb_i[:, :, :], 7, None, ALU.arith_shift_right))
                    link(V.tensor_copy(nb_f[:, :, :], nb_i[:, :, :]))
                    link(V.tensor_tensor(chunks[:, :], nb_f[:, 0, :], nb_f[:, 1, :], ALU.max))
                    link(V.tensor_scalar(chunks[:, :], chunks[:, :], 1.0, None, ALU.max))
                    link(V.tensor_reduce(red[:, 4:5], chunks[:, :], AX, ALU.max))

                V.memset(red[:, 5:6], 0.0).then_inc(rank_sems[0]["zero"], 1)
                rank(rank_sems[0], s_chain[0])
                v.wait_ge(rank_sems[0]["last"], trips * (4 * U))
                counts()
                V.tensor_copy(kept_i[:, 2:3], red[:, 4:5]).then_inc(s_rmax, 1)
                v.wait_ge(s_rmax, 1)
                rmax = v.value_load(kept_i[0:1, 2:3], min_val=1, max_val=ROUNDS)
                with v.If(rmax > 1):
                    for h in range(2):
                        v.wait_ge(rank_sems[0]["scat"][h], trips * (2 * U * 16))
                    V.memset(red[:, 5:6], 0.0).then_inc(rank_sems[1]["zero"], 1)
                    rank(rank_sems[1], s_chain[1])
                link(V.tensor_tensor_scan(out=ends[:, :], data0=ones_c[:, 0:G], data1=chunks[:, :], initial=0.0, op0=ALU.mult, op1=ALU.add))
                for c in range(TC):
                    link(V.tensor_scalar(hit[:, :], ends[:, :], iota_t[:, c:c + 1], 0.0, ALU.is_le, ALU.add, accum_out=tt[:, 0, c:c + 1]))
                    link(V.tensor_tensor_reduce(prod[:, 0, :], hit[:, :], chunks[:, :], 1.0, 0.0, ALU.mult, ALU.add, tt[:, 1, c:c + 1]))
                link(V.tensor_tensor(tt[:, 2, :], iota_t[:, :], tt[:, 1, :], ALU.subtract))
                link(V.tensor_scalar(tt[:, 4, :], tt[:, 0, :], float(GROUP), None, ALU.mult))
                link(V.tensor_scalar(tf[:, 0, :], tt[:, 0, :], float(GROUP), -1.0, ALU.mult, ALU.add))
                link(V.tensor_scalar(tf[:, 1, :], tt[:, 2, :], 0.0, None, ALU.is_gt))
                link(V.tensor_scalar(tf[:, 2, :], tt[:, 2, :], 0.0, -BIG, ALU.is_le, ALU.mult))
                link(V.scalar_tensor_tensor(out=tt[:, 6, :], in0=tt[:, 2, :], scalar=float(G), in1=tt[:, 0, :], op0=ALU.mult, op1=ALU.add))
                link(V.tensor_scalar(tt[:, 7, :], tt[:, 0, :], float(G - 1), None, ALU.is_gt))
                link(V.tensor_scalar(tt[:, 2, :], tt[:, 6, :], -1.0, float(CHUNKS), ALU.mult, ALU.add))
                link(V.tensor_tensor(tt[:, 2, :], tt[:, 2, :], tt[:, 7, :], ALU.mult))
                link(V.tensor_tensor(tt[:, 6, :], tt[:, 6, :], tt[:, 2, :], ALU.add))
                link(V.tensor_copy(ti[:, 0, :], tt[:, 4, :]))
                link(V.tensor_copy(rounds_i[:, :], red[:, 4:5]))
                link(V.tensor_copy(ti[:, 1, :], tt[:, 6, :]))
                link(V.tensor_scalar(kept_i[:, 4:5], ends[:, G - 1:G], float(UN), None, ALU.add))
                link(V.tensor_scalar(kept_i[:, 5:6], kept_i[:, 4:5], UN.bit_length() - 1, None, ALU.arith_shift_right))
                link(V.tensor_scalar(n_turns[:, 0:1], kept_i[:, 5:6], -float(PEEL), None, ALU.add))
                V.tensor_scalar(tf[:, 3, :], tf[:, 1, :], 0.0, looped[:, :], ALU.is_equal, ALU.mult).then_inc(s_tab, 1)

        shared = dict(G=G, TMAX=TMAX, ROUNDS=ROUNDS, CHUNKS=CHUNKS, weights=weights, lists=lists, x=x, out=out, ctx=ctx,
                      x1_dram=x1_dram, h1_dram=h1_dram, step_row=step_row, step_f=step_f, ones_f=ones_f, ones_b=ones_b,
                      ident_f=ident_f, n_turns=n_turns, looped=looped, rounds_i=rounds_i)
        layer_max(nc, shared)
        layer_gru(nc, shared)


def layer_max(nc, shared):
    G, TMAX, weights, lists = (shared[k] for k in ("G", "TMAX", "weights", "lists"))
    x, x1_dram, h1_dram, step_row, step_f = (shared[k] for k in ("x", "x1_dram", "h1_dram", "step_row", "step_f"))
    ones_f, ones_b, ident_f, n_turns, looped, rounds_i = (shared[k] for k in ("ones_f", "ones_b", "ident_f", "n_turns", "looped", "rounds_i"))
    NPAD = (G + 1) * GROUP
    max_turns = TMAX // UN - PEEL

    with ExitStack() as ctx:
        def sb(name, shape, dt=F32):
            return ctx.enter_context(nc.sbuf_tensor(name, shape, dt))

        def ps(name, shape, dt=F32):
            return ctx.enter_context(nc.psum_tensor(name, shape, dt))

        def sem(name):
            return shared["ctx"].enter_context(nc.semaphore(name))

        w1a = sb("w1a", [P, D])
        w1b = sb("w1b", [P, D])
        w2 = sb("w2", [P, D])
        b1 = sb("b1", [P, 1])
        b2 = sb("b2", [P, 1])
        w1d = sb("w1d", [P, D])
        b1_own = sb("b1_own", [P, 1])
        no_own = sb("no_own", [P, 1])
        gap = sb("gap", [P, 1])
        eps = sb("eps", [P, 1])
        rounds_f = sb("rounds_f", [P, 1])
        general_f = sb("general_f", [P, 1])
        general_i = sb("general_i", [P, 1], I32)
        ones_h = sb("ones_h", [P, P], F16)
        ident_h = sb("ident_h", [P, P], F16)
        half_before = sb("half_before", [P, P], F16)
        iota_n = sb("iota_n", [P, P + 2])
        iota_loc = sb("iota_loc", [P, TILES, P], F16)

        ent = sb("ent", [P, UN, 4], F16)
        rep = sb("rep", [P, 2, P], F16)
        junk = sb("junk", [P, 2, P])
        rank = sb("rank", [P, 2])
        place = sb("place", [P, 2, P + 2], F16)
        dplace = sb("dplace", [P, 2, P + 1], F16)
        sorted4 = sb("sorted4", [P, 2, 4])
        reset = sb("reset", [P, UN, P])
        idx = sb("idx", [P, 4, 2], I32)
        last_loc = sb("last_loc", [P, UN, 1])
        carry = sb("carry", [P, 1])
        x3 = sb("x3", [P, UN, TILES, D])
        xg = sb("xg", [P, 4, 2, D])
        stats = sb("stats", [P, 2, 5, 6])
        mv = sb("mv", [P, 2, 5, 2])
        std = sb("std", [P, 2, 5])
        rs = sb("rs", [P, 4, 5])
        nm = sb("nm", [P, 4, 5])
        h = sb("h", [P, 2, 5, D])
        hT = sb("hT", [P, 2, 5 * P])
        hid = sb("hid", [P, 4, 5 * P])
        runmax = sb("runmax", [P, 2, P])
        reached = sb("reached", [P, 2, P])
        gain = sb("gain", [P, 2, P])
        part = sb("part", [P, 2, 3, D], BF16)
        rest = sb("rest", [P, 2, D])
        onehot = sb("onehot", [P, 2, GROUP], BF16)
        resT = sb("resT", [P, 2, GROUP])
        absent = sb("absent", [P, GROUP])
        found = sb("found", [P, GROUP])
        kept = sb("kept_max", [P, 2, GROUP])
        present = sb("present", [P, GROUP])
        clean = sb("clean", [P, GROUP])
        x1s = sb("x1s", [P, 4, GROUP])
        stats1 = sb("stats1", [P, 2, 3, 6])
        mv1 = sb("mv1", [P, 2, 3, 2])
        std1 = sb("std1", [P, 2, 3])
        rs1 = sb("rs1", [P, 2, 3])
        nm1 = sb("nm1", [P, 2, 3])
        h1s = sb("h1s", [P, 4, GROUP])

        ps_k = ps("ps_k", [P, 512])
        ps_t = ps("ps_t", [P, 512])
        ps_e = ps("ps_e", [P, 512])
        ps_h = ps("ps_h", [P, 512])
        ps_m = ps("ps_m", [P, 512])
        ps_g = ps("ps_g", [P, 512])
        ps_x = ps("ps_x", [P, 512])
        ps_o = ps("ps_o", [P, 512])

        names = ("weights const prep rep key rank pe dp sorted srt idx bn mv std rs h hg tn te hT hidep hide msge "
                 "scan most gain scT hi r1 mid lo oh seen t1 t2 cont ext res O x1 bn1 mv1 std1 rs1 h1 present clean carry go").split()
        S = {n: sem(f"a_{n}") for n in names}
        d_ent, d_x, d_gat = ([sem(f"a_{n}{q}") for q in range(4)] for n in ("ent_in", "x_in", "gathered"))
        d_x1, d_h1 = ([sem(f"a_{n}{q}") for q in range(2)] for n in ("x1_out", "h1_out"))

        block = ctx.enter_context(nc.Block())

        def turns_of(eng):
            return eng.value_load(n_turns[0:1, 0:1], min_val=1, max_val=max_turns)

        def after(eng, name, st, per=1, back=0):
            if st.past(back):
                eng.wait_ge(S[name], st.count(per, back))

        def landed(eng, sems, st, back=0, per=16):
            if st.past(back):
                eng.wait_ge(sems[st.slot(len(sems), back)], st.landed(len(sems), back, per))

        @block.sync
        def _(sp):
            for tile, src in ((w1a, weights["W1"][0:D, :]), (w1b, weights["W1"][D:2 * D, :]), (w2, weights["W2"]),
                              (b1, weights["b1"].rearrange("(p o) -> p o", o=1)), (b2, weights["b2"].rearrange("(p o) -> p o", o=1))):
                sp.dma_start(tile[:, :], src).then_inc(S["weights"], 16)
            sp.wait_ge(S["weights"], 5 * 16)
            turns = turns_of(sp)

            def entries_in(st):
                chunk = sp.value_load(step_row[0:1, 1, bass.ds(st.t, 1)], min_val=0, max_val=shared["CHUNKS"])
                after(sp, "rep", st, back=4)
                sp.sem_inc(S["go"], 1)
                after(sp, "sorted", st, back=UN)
                sp.dma_start(ent[:, st.slot(UN), :], lists[0][bass.ds(chunk * P, P), :]).then_inc(d_ent[st.slot(4)], 16)

            def x_in(st):
                base = sp.value_load(step_row[0:1, 0, bass.ds(st.t, 1)], min_val=0, max_val=NPAD - GROUP)
                after(sp, "x1", st, back=UN)
                sp.dma_start(x3[:, st.slot(UN), :, :],
                             x[bass.ds(base, GROUP), :].rearrange("(p t) d -> p t d", t=TILES)).then_inc(d_x[st.slot(4)], 16)

            def rows_out(st):
                base = sp.value_load(step_row[0:1, 0, bass.ds(st.t, 1)], min_val=0, max_val=NPAD - GROUP)
                for name, sems, tile, dram in (("x1", d_x1, x1s, x1_dram), ("h1", d_h1, h1s, h1_dram)):
                    after(sp, name, st, per=1 if name == "x1" else 3)
                    landed(sp, sems, st, back=1)
                    sp.dma_start(dram[bass.ds(base, GROUP), :].rearrange("(p t) d -> p (t d)", t=TILES),
                                 tile[:, st.slot(4), :]).then_inc(sems[st.slot(2)], 16)

            loop(sp, turns, [(0, entries_in), (6, x_in), (15, rows_out)])
            for sems in (d_x1, d_h1):
                landed(sp, sems, Step(turns, PEEL * UN - 1))
                sp.sem_inc(S["carry"], 1)

        @block.gpsimd
        def _(pool):
            G_ = nc.gpsimd
            G_.iota(iota_n[:, :], pattern=[[1, P + 2]], base=-1, channel_multiplier=0, allow_small_or_imprecise_dtypes=True).then_inc(S["const"], 1)
            G_.iota(iota_loc[:, :, :], pattern=[[1, TILES], [TILES, P]], base=1, channel_multiplier=0,
                    allow_small_or_imprecise_dtypes=True).then_inc(S["const"], 1)
            G_.memset(ones_h[:, :], 1.0).then_inc(S["const"], 1)
            G_.memset(eps[:, :], EPS).then_inc(S["const"], 1)
            G_.memset(half_before[:, :], -0.5).then_inc(S["const"], 1)
            G_.memset(kept[:, :, :], 0.0).then_inc(S["const"], 1)
            pool.wait_ge(S["const"], 6)
            G_.affine_select(out=half_before[:, :], in_=half_before[:, :], compare_op=ALU.is_gt, fill=0.0, base=0,
                             pattern=[[-1, P]], channel_multiplier=1).then_inc(S["const"], 1)
            G_.affine_select(out=ident_h[:, :], in_=ones_h[:, :], compare_op=ALU.is_equal, fill=0.0, base=0,
                             pattern=[[-1, P]], channel_multiplier=1).then_inc(S["const"], 1)
            turns = turns_of(pool)

            def gather(st):
                after(pool, "idx", st, per=3)
                after(pool, "hg", st, per=3, back=4)
                pool.sem_inc(S["go"], 1)
                for q in range(2):
                    G_.indirect_dma_start(out=xg[:, st.slot(4), q, :], out_offset=None, in_=x[:, :],
                                          in_offset=bass.IndirectOffsetOnAxis(ap=idx[:, st.slot(4), q:q + 1], axis=0)
                                          ).then_inc(d_gat[st.slot(4)], 16)

            def low_part(st):
                after(pool, "mid", st)
                after(pool, "ext", st, back=2)
                G_.tensor_tensor(part[:, st.slot(2), 2, :], rest[:, st.slot(2), :], part[:, st.slot(2), 1, :], ALU.subtract).then_inc(S["lo"], 1)

            def normalize(st):
                after(pool, "rs", st, per=2)
                after(pool, "te", st, back=2)
                pool.sem_inc(S["go"], 1)
                for q in range(TILES - 1, TILES + 2):
                    rows = x3[:, st.slot(UN), q, :] if q < TILES else xg[:, st.slot(4), q - TILES, :]
                    G_.tensor_scalar(h[:, st.slot(2), q, :], rows, rs[:, st.slot(4), q:q + 1], nm[:, st.slot(4), q:q + 1],
                                     ALU.mult, ALU.add).then_inc(S["hg"], 1)

            def repeat_places(st):
                landed(pool, d_ent, st)
                after(pool, "sorted", st, back=2)
                pool.sem_inc(S["go"], 1)
                G_.tensor_scalar(rep[:, st.slot(2), :], ones_h[:, :], ent[:, st.slot(UN), 2:3], None, ALU.mult).then_inc(S["rep"], 1)

            def lane_changes(st):
                after(pool, "pe", st)
                after(pool, "sorted", st, back=2)
                G_.tensor_tensor(dplace[:, st.slot(2), :], place[:, st.slot(2), 1:P + 2], place[:, st.slot(2), 0:P + 1],
                                 ALU.subtract).then_inc(S["dp"], 1)

            loop(pool, turns, [(6, gather), (8, normalize), (11, low_part), (2, repeat_places), (3, lane_changes)])

        @block.scalar
        def _(act):
            A = nc.scalar
            turns = turns_of(act)
            act.wait_ge(S["weights"], 5 * 16)
            act.wait_ge(S["const"], 8)
            act.wait_ge(S["prep"], 8)
            general = act.value_load(general_i[0:1, 0:1], min_val=0, max_val=1)

            def deviation(st):
                after(act, "mv", st, per=5)
                after(act, "rs", st, per=2, back=2)
                A.activation(std[:, st.slot(2), :], mv[:, st.slot(2), :, 1], ACT.Sqrt, bias=eps[:, :]).then_inc(S["std"], 1)

            def normalize(st):
                after(act, "rs", st, per=2)
                after(act, "tn", st, back=2)
                for q in range(TILES - 1):
                    A.activation(h[:, st.slot(2), q, :], x3[:, st.slot(UN), q, :], ACT.Identity, bias=nm[:, st.slot(4), q:q + 1],
                                 scale=rs[:, st.slot(4), q:q + 1]).then_inc(S["h"], 1)

            def columns(st):
                after(act, "tn", st)
                after(act, "hidep", st, back=2)
                A.activation(hT[:, st.slot(2), 0:4 * P], ps_t[:, :], ACT.Relu).then_inc(S["hT"], 1)
                after(act, "te", st)
                A.activation(hT[:, st.slot(2), 4 * P:5 * P], ps_e[:, 0:P], ACT.Relu).then_inc(S["hT"], 1)

            def sorted_edges(st):
                after(act, "sorted", st)
                after(act, "idx", st, per=3, back=2)
                A.copy(sorted4[:, st.slot(2), :], ps_k[:, 256:260]).then_inc(S["srt"], 1)
                after(act, "scan", st, back=UN)
                A.activation(reset[:, st.slot(UN), :], ps_k[:, P:2 * P], ACT.Copy, scale=-RESET).then_inc(S["srt"], 1)

            def hidden(st):
                after(act, "hidep", st)
                after(act, "ext", st, back=4)
                A.activation(hid[:, st.slot(4), 0:4 * P], ps_h[:, :], ACT.Relu, bias=b1_own[:, :], scale=looped[:, :]).then_inc(S["hide"], 1)
                A.activation(hid[:, st.slot(4), 4 * P:5 * P], ps_e[:, P:2 * P], ACT.Relu, bias=b1[:, :]).then_inc(S["hide"], 1)

            def high_part(st):
                after(act, "scT", st)
                after(act, "ext", st, back=2)
                A.copy(part[:, st.slot(2), 0, :], ps_g[:, 0:P]).then_inc(S["hi"], 1)

            def middle_part(st):
                after(act, "r1", st)
                A.copy(part[:, st.slot(2), 1, :], rest[:, st.slot(2), :]).then_inc(S["mid"], 1)

            def results(st):
                after(act, "ext", st)
                after(act, "O", st, back=2)
                A.activation(resT[:, st.slot(2), :], ps_x[:, 0:GROUP], ACT.Identity, bias=b2[:, :]).then_inc(S["res"], 1)

            def absence(st):
                with act.If(general > 0):
                    after(act, "seen", st)
                    after(act, "t2", st, back=1)
                    A.activation(absent[:, :], ps_o[:, 0:GROUP], ACT.Identity, bias=no_own[:, :], scale=gap[:, :]).then_inc(S["t1"], 1)

            def deviation1(st):
                after(act, "mv1", st, per=3)
                after(act, "rs1", st, per=2, back=2)
                A.activation(std1[:, st.slot(2), :], mv1[:, st.slot(2), :, 1], ACT.Sqrt, bias=eps[:, :]).then_inc(S["std1"], 1)

            def normalize1(st):
                after(act, "rs1", st, per=2)
                landed(act, d_h1, st, back=4)
                for q in range(3):
                    A.activation(h1s[:, st.slot(4), q * D:(q + 1) * D], x1s[:, st.slot(4), q * D:(q + 1) * D], ACT.Relu,
                                 bias=nm1[:, st.slot(2), q:q + 1], scale=rs1[:, st.slot(2), q:q + 1]).then_inc(S["h1"], 1)

            loop(act, turns, [(11, high_part), (8, deviation), (14, deviation1), (12, results), (9, columns), (4, sorted_edges), (8, normalize), (11, middle_part),
                              (14, normalize1), (9, hidden), (12, absence)])

        @block.tensor
        def _(pe):
            T = nc.tensor
            turns = turns_of(pe)
            pe.wait_ge(S["weights"], 5 * 16)
            pe.wait_ge(S["const"], 8)
            pe.wait_ge(S["prep"], 8)
            general = pe.value_load(general_i[0:1, 0:1], min_val=0, max_val=1)

            def keys(st):
                after(pe, "rep", st)
                after(pe, "srt", st, per=2, back=1)
                T.matmul(ps_k[:, 0:P], rep[:, st.slot(2), :], ident_h[:, :], start=True, stop=False)
                T.matmul(ps_k[:, 0:P], ident_h[:, :], half_before[:, :], start=False, stop=True).then_inc(S["key"], 1)

            def sort(st):
                after(pe, "dp", st)
                landed(pe, d_ent, st)
                after(pe, "rank", st)
                s2, e4 = st.slot(2), ent[:, st.slot(UN), :]
                T.matmul(ps_k[:, 256:259], place[:, s2, 1:P + 1], e4[:, 0:3], start=True, stop=True)
                T.matmul(ps_k[:, 259:260], dplace[:, s2, 1:P + 1], e4[:, 2:3], start=True, stop=True)
                T.matmul(ps_k[:, P:2 * P], rep[:, s2, :], dplace[:, s2, 0:P], start=True, stop=True).then_inc(S["sorted"], 1)

            def turn_rows(st):
                after(pe, "h", st, per=TILES - 1)
                after(pe, "hg", st, per=3)
                after(pe, "hT", st, per=2, back=1)
                for q in range(4):
                    mm = T.transpose(ps_t[:, q * P:(q + 1) * P], h[:, st.slot(2), (0, 1, 2, 4)[q], :], ident_f[:, :])
                mm.then_inc(S["tn"], 1)
                after(pe, "hide", st, per=2, back=1)
                T.transpose(ps_e[:, 0:P], h[:, st.slot(2), 3, :], ident_f[:, :]).then_inc(S["te"], 1)

            def mlp(st):
                after(pe, "hT", st, per=2)
                after(pe, "hide", st, per=2, back=1)
                s2 = st.slot(2)
                T.matmul(ps_h[:, :], w1a[:, :], hT[:, s2, 0:4 * P], start=True, stop=True)
                T.matmul(ps_e[:, P:2 * P], w1d[:, :], hT[:, s2, 3 * P:4 * P], start=True, stop=False)
                T.matmul(ps_e[:, P:2 * P], w1b[:, :], hT[:, s2, 4 * P:5 * P], start=False, stop=True).then_inc(S["hidep"], 1)

            def messages(st):
                after(pe, "hide", st, per=2)
                after(pe, "gain", st, back=1)
                T.matmul(ps_m[:, 0:2 * P], w2[:, :], hid[:, st.slot(4), 3 * P:5 * P], start=True, stop=True).then_inc(S["msge"], 1)

            def turn_gains(st):
                after(pe, "gain", st)
                after(pe, "hi", st, back=1)
                after(pe, "r1", st, back=1)
                T.transpose(ps_g[:, 0:P], gain[:, st.slot(2), :], ident_f[:, :]).then_inc(S["scT"], 1)

            def spread(st):
                after(pe, "lo", st)
                after(pe, "oh", st)
                after(pe, "res", st, back=1)
                T.matmul(ps_x[:, 0:GROUP], w2[:, :], hid[:, st.slot(4), 0:GROUP], start=True, stop=False)
                for q in range(3):
                    mm = T.matmul(ps_x[:, 0:GROUP], part[:, st.slot(2), q, :], onehot[:, st.slot(2), :], start=False, stop=(q == 2))
                mm.then_inc(S["ext"], 1)

            def turn_results(st):
                after(pe, "x1", st, back=1)
                pe.sem_inc(S["go"], 1)
                with pe.If(general > 0):
                    T.matmul(ps_o[:, 0:GROUP], ones_b[:, :], onehot[:, st.slot(2), :], start=True, stop=True).then_inc(S["seen"], 1)
                    after(pe, "t1", st)
                    after(pe, "clean", st)
                    for q in range(3):
                        mm = T.transpose(ps_o[:, q * P:(q + 1) * P], clean[:, q * P:(q + 1) * P], ident_f[:, :])
                    mm.then_inc(S["O"], 1)
                with pe.Else():
                    after(pe, "res", st)
                    for q in range(3):
                        mm = T.transpose(ps_o[:, q * P:(q + 1) * P], resT[:, st.slot(2), q * P:(q + 1) * P], ident_f[:, :])
                    mm.then_inc(S["O"], 1)

            loop(pe, turns, [(12, spread), (9, turn_rows), (10, messages), (4, sort), (9, mlp), (3, keys), (10, turn_gains), (12, turn_results)])

        @block.vector
        def _(v):
            V = nc.vector
            done = [0]

            def link(ins):
                done[0] += 1
                ins.then_inc(S["prep"], 1)
                v.wait_ge(S["prep"], done[0])

            v.wait_ge(S["weights"], 5 * 16)
            v.wait_ge(S["const"], 8)
            link(V.tensor_scalar(no_own[:, :], looped[:, :], -1.0, BIG, ALU.add, ALU.mult))
            link(V.tensor_scalar(gap[:, :], no_own[:, :], -1.0, None, ALU.mult))
            link(V.tensor_tensor(b1_own[:, :], b1[:, :], looped[:, :], ALU.mult))
            link(V.tensor_tensor(w1d[:, :], w1a[:, :], w1b[:, :], ALU.subtract))
            link(V.tensor_copy(rounds_f[:, :], rounds_i[:, :]))
            link(V.tensor_scalar(rounds_f[:, :], rounds_f[:, :], 1.5, None, ALU.is_gt))
            link(V.tensor_scalar(general_f[:, :], looped[:, :], 0.0, rounds_f[:, :], ALU.is_equal, ALU.max))
            link(V.tensor_copy(general_i[:, :], general_f[:, :]))
            turns = turns_of(v)
            general = v.value_load(general_i[0:1, 0:1], min_val=0, max_val=1)

            def rank_edges(st):
                s2 = st.slot(2)
                after(v, "key", st)
                after(v, "pe", st, back=2)
                V.tensor_scalar(junk[:, s2, :], ps_k[:, 0:P], ent[:, st.slot(UN), 2:3], 0.0, ALU.is_lt, ALU.add,
                                accum_out=rank[:, s2:s2 + 1]).then_inc(S["rank"], 1)

            def lanes(st):
                s2 = st.slot(2)
                after(v, "rank", st)
                after(v, "sorted", st, back=2)
                after(v, "dp", st, back=2)
                V.tensor_scalar(place[:, s2, :], iota_n[:, :], rank[:, s2:s2 + 1], None, ALU.is_equal).then_inc(S["pe"], 1)

            def row_numbers(st):
                s2 = st.slot(2)
                after(v, "srt", st, per=2)
                landed(v, d_gat, st, back=4, per=32)
                V.scalar_tensor_tensor(out=idx[:, st.slot(4), 0:1], in0=sorted4[:, s2, 0:1], scalar=256.0, in1=sorted4[:, s2, 1:2],
                                       op0=ALU.mult, op1=ALU.add).then_inc(S["idx"], 1)
                V.tensor_scalar(idx[:, st.slot(4), 1:2], sorted4[:, s2, 2:3], step_f[:, 0, bass.ds(st.t, 1)], float(NPAD - 1),
                                ALU.add, ALU.min).then_inc(S["idx"], 1)
                after(v, "oh", st, back=UN)
                V.scalar_tensor_tensor(out=last_loc[:, st.slot(UN), :], in0=sorted4[:, s2, 3:4], scalar=0.0, in1=sorted4[:, s2, 2:3],
                                       op0=ALU.not_equal, op1=ALU.mult).then_inc(S["idx"], 1)

            def statistics(st):
                s2 = st.slot(2)
                landed(v, d_x, st)
                landed(v, d_gat, st, per=32)
                after(v, "mv", st, per=5, back=2)
                for q in range(5):
                    rows = x3[:, st.slot(UN), q, :] if q < 3 else xg[:, st.slot(4), q - 3, :]
                    V.bn_stats(stats[:, s2, q, :], rows).then_inc(S["bn"], 1)

            def averages(st):
                after(v, "bn", st, per=5)
                after(v, "std", st, back=2)
                v.sem_inc(S["go"], 1)
                for q in range(5):
                    V.bn_aggr(mv[:, st.slot(2), q, :], stats[:, st.slot(2), q, :]).then_inc(S["mv"], 1)

            def scales(st):
                after(v, "std", st)
                after(v, "h", st, per=TILES - 1, back=4)
                after(v, "hg", st, per=3, back=4)
                V.reciprocal(rs[:, st.slot(4), :], std[:, st.slot(2), :]).then_inc(S["rs"], 1)

            def shifts(st):
                v.wait_ge(S["rs"], st.count(2) - 1)
                V.scalar_tensor_tensor(out=nm[:, st.slot(4), :], in0=mv[:, st.slot(2), :, 0], scalar=-1.0, in1=rs[:, st.slot(4), :],
                                       op0=ALU.mult, op1=ALU.mult).then_inc(S["rs"], 1)

            def run_maximum(st):
                after(v, "msge", st)
                after(v, "most", st, back=2)
                V.tensor_tensor_scan(out=runmax[:, st.slot(2), :], data0=reset[:, st.slot(UN), :], data1=ps_m[:, P:2 * P],
                                     initial=0.0, op0=ALU.add, op1=ALU.max).then_inc(S["scan"], 1)

            def with_own(st):
                after(v, "scan", st)
                after(v, "gain", st, back=2)
                V.scalar_tensor_tensor(out=reached[:, st.slot(2), :], in0=ps_m[:, 0:P], scalar=no_own[:, :], in1=runmax[:, st.slot(2), :],
                                       op0=ALU.add, op1=ALU.max).then_inc(S["most"], 1)

            def gains(st):
                after(v, "most", st)
                after(v, "scT", st, back=2)
                V.tensor_tensor(gain[:, st.slot(2), :], reached[:, st.slot(2), :], ps_m[:, 0:P], ALU.subtract).then_inc(S["gain"], 1)

            def remainder(st):
                after(v, "hi", st)
                after(v, "lo", st, back=2)
                V.tensor_tensor(rest[:, st.slot(2), :], ps_g[:, 0:P], part[:, st.slot(2), 0, :], ALU.subtract).then_inc(S["r1"], 1)

            def one_hot(st):
                after(v, "ext", st, back=2)
                V.tensor_scalar(onehot[:, st.slot(2), :], iota_loc[:, :, :].rearrange("p t r -> p (t r)"), last_loc[:, st.slot(UN), :],
                                None, ALU.is_equal).then_inc(S["oh"], 1)

            def chunk_maximum(st):
                with v.If(general > 0):
                    after(v, "res", st)
                    after(v, "t1", st)
                    after(v, "carry", st, back=1)
                    V.tensor_copy(carry[:, :], step_f[:, 2, bass.ds(st.t, 1)]).then_inc(S["carry"], 1)
                    after(v, "cont", st, back=1)
                    V.tensor_tensor(found[:, :], resT[:, st.slot(2), :], absent[:, :], ALU.add).then_inc(S["t2"], 1)
                    after(v, "t2", st)
                    after(v, "carry", st)
                    V.scalar_tensor_tensor(out=kept[:, st.slot(2), :], in0=kept[:, st.slot(2, 1), :], scalar=carry[:, :],
                                           in1=found[:, :], op0=ALU.add, op1=ALU.max).then_inc(S["cont"], 1)
                    after(v, "cont", st)
                    after(v, "clean", st, back=1)
                    V.tensor_scalar(present[:, :], kept[:, st.slot(2), :], -BIG / 2, None, ALU.is_gt).then_inc(S["present"], 1)
                    after(v, "present", st)
                    after(v, "O", st, back=1)
                    V.tensor_tensor(clean[:, :], kept[:, st.slot(2), :], present[:, :], ALU.mult).then_inc(S["clean"], 1)

            def add_x(st):
                x_rows = x3[:, st.slot(UN), :, :].rearrange("p t d -> p (t d)")
                after(v, "O", st)
                landed(v, d_x1, st, back=4)
                after(v, "h1", st, per=3, back=4)
                V.tensor_tensor(x1s[:, st.slot(4), :], x_rows, ps_o[:, 0:GROUP], ALU.add).then_inc(S["x1"], 1)

            def statistics1(st):
                after(v, "x1", st)
                after(v, "mv1", st, per=3, back=2)
                for q in range(3):
                    V.bn_stats(stats1[:, st.slot(2), q, :], x1s[:, st.slot(4), q * D:(q + 1) * D]).then_inc(S["bn1"], 1)

            def averages1(st):
                after(v, "bn1", st, per=3)
                after(v, "std1", st, back=2)
                v.sem_inc(S["go"], 1)
                for q in range(3):
                    V.bn_aggr(mv1[:, st.slot(2), q, :], stats1[:, st.slot(2), q, :]).then_inc(S["mv1"], 1)

            def scales1(st):
                after(v, "std1", st)
                after(v, "h1", st, per=3, back=2)
                V.reciprocal(rs1[:, st.slot(2), :], std1[:, st.slot(2), :]).then_inc(S["rs1"], 1)

            def shifts1(st):
                v.wait_ge(S["rs1"], st.count(2) - 1)
                V.scalar_tensor_tensor(out=nm1[:, st.slot(2), :], in0=mv1[:, st.slot(2), :, 0], scalar=-1.0, in1=rs1[:, st.slot(2), :],
                                       op0=ALU.mult, op1=ALU.mult).then_inc(S["rs1"], 1)

            loop(v, turns, [(13, add_x), (8, scales), (11, remainder), (8, shifts), (13, statistics1), (14, scales1), (13, averages1),
                            (14, shifts1), (10, run_maximum), (11, one_hot), (10, with_own), (5, row_numbers), (10, gains),
                            (12, chunk_maximum), (7, statistics), (3, rank_edges), (7, averages), (3, lanes)])


def layer_gru(nc, shared):
    G, TMAX, weights, lists, out = (shared[k] for k in ("G", "TMAX", "weights", "lists", "out"))
    x1_dram, h1_dram, step_row, step_f = (shared[k] for k in ("x1_dram", "h1_dram", "step_row", "step_f"))
    ones_b, ident_f, n_turns, looped, rounds_i = (shared[k] for k in ("ones_b", "ident_f", "n_turns", "looped", "rounds_i"))
    NPAD = (G + 1) * GROUP
    H3 = 3 * D
    max_turns = TMAX // UN - PEEL

    with ExitStack() as ctx:
        def sb(name, shape, dt=F32):
            return ctx.enter_context(nc.sbuf_tensor("g_" + name, shape, dt))

        def ps(name):
            return ctx.enter_context(nc.psum_tensor("gp_" + name, [P, 512], F32))

        w_in = sb("w_in", [P, D])
        w_out = sb("w_out", [P, D])
        w_ih = sb("w_ih", [P, 3, 2 * D])
        w_hh = sb("w_hh", [P, 3, D])
        w_ihT = sb("w_ihT", [P, 2, H3])
        lhs = sb("lhs", [P, 3, H3])
        wp = sb("wp", [P, 2, 3, H3], F16)
        wmax = sb("wmax", [P, 4])
        wexp = sb("wexp", [P, 1], I32)
        scale = sb("scale", [P, 1])
        unscale = sb("unscale", [P, 1])
        b_side = sb("b_side", [P, 2])
        b_ih = sb("b_ih", [P, 3])
        b_hh = sb("b_hh", [P, 3])
        b_gate = sb("b_gate", [P, 4])
        c_gate = sb("c_gate", [P, 2, 3])
        c_sum = sb("c_sum", [P, 3])
        c_pick = sb("c_pick", [P, 2, TILES, 2 * TILES])
        c_rows = sb("c_rows", [2 * TILES, TILES, H3])
        looped_i = sb("looped_i", [P, 1], I32)
        iota_loc = sb("iota_loc", [P, TILES, P], F16)

        ent = sb("ent", [P, UN, 2, 4], F16)
        idx = sb("idx", [P, 4, 2], I32)
        rows = sb("rows", [P, 4, 2, D])
        part = sb("part", [P, 4, 2, 2, D], F16)
        onehot = sb("onehot", [P, 2, 2, GROUP], F16)
        ones_h = sb("ones_h", [P, 1], F16)
        h_rows = sb("h_rows", [P, 4, TILES * D])
        x_rows = sb("x_rows", [P, 4, TILES * D])
        hT = sb("hT", [P, UN, GROUP])
        sums = sb("sums", [P, 2, 2, GROUP])
        fresh = sb("fresh", [P, 2, GROUP])
        edges = sb("edges", [P, 2, 2, TILES])
        count = sb("count", [P, 2, 2, TILES])
        share = sb("share", [P, 2, 2, TILES])
        mean = sb("mean", [P, 2, 2 * GROUP + P])
        mT = sb("mT", [P, 2, 2, 2, GROUP], F16)
        hp = sb("hp", [P, 2, 2, GROUP], F16)
        none = sb("none", [2 * TILES, 2, P])
        r = sb("r", [P, 2, GROUP])
        z = sb("z", [P, 4, GROUP])
        rh = sb("rh", [P, 2, GROUP])
        pre = sb("pre", [P, 2, GROUP])
        n = sb("n", [P, 4, GROUP])
        d = sb("d", [P, 2, GROUP])
        e = sb("e", [P, 2, GROUP])
        f = sb("f", [P, 2, GROUP])
        out_rows = sb("out_rows", [P, 4, GROUP])

        ps_s0, ps_s1, ps_r, ps_z, ps_nh, ps_ni, ps_t, ps_o = (ps(q) for q in ("s0", "s1", "r", "z", "nh", "ni", "t", "o"))
        ps_s = (ps_s0, ps_s1)

        names = ("weights const prep turned wcopy idx high low oh agg edges sum fresh count share mean tn tm0 tm1 hT hh hl mh0 mh1 ml0 ml1 "
                 "rg zg nhg nig r z rh pre n d e f to out none go").split()
        S = {q: shared["ctx"].enter_context(nc.semaphore(f"g_{q}")) for q in names}
        d_ent, d_gat, d_h, d_x, d_out = ([shared["ctx"].enter_context(nc.semaphore(f"g_{q}{k}")) for k in range(depth)]
                                         for q, depth in (("ent_in", 4), ("gathered", 4), ("h_in", 4), ("x_in", 4), ("rows_out", 2)))
        block = ctx.enter_context(nc.Block())
        N_LOADS = 6 + 6

        def turns_of(eng):
            return eng.value_load(n_turns[0:1, 0:1], min_val=1, max_val=max_turns)

        def after(eng, name, st, per=1, back=0):
            if st.past(back):
                eng.wait_ge(S[name], st.count(per, back))

        def landed(eng, sems, st, back=0, per=16):
            if st.past(back):
                eng.wait_ge(sems[st.slot(len(sems), back)], st.landed(len(sems), back, per))

        @block.sync
        def _(sp):
            def load(tile, src):
                sp.dma_start(tile, src).then_inc(S["weights"], 16)

            load(w_in[:, :], weights["W_in"])
            load(w_out[:, :], weights["W_out"])
            load(w_ih[:, :, :], weights["w_ih"].rearrange("(g p) j -> p g j", p=P))
            load(w_hh[:, :, :], weights["w_hh"].rearrange("(g p) j -> p g j", p=P))
            load(b_side[:, 0:1], weights["b_in"].rearrange("(p o) -> p o", o=1))
            load(b_side[:, 1:2], weights["b_out"].rearrange("(p o) -> p o", o=1))
            for tile, name in ((b_ih, "b_ih"), (b_hh, "b_hh")):
                for g in range(3):
                    load(tile[:, g:g + 1], weights[name][g * D:(g + 1) * D].rearrange("(p o) -> p o", o=1))
            sp.wait_ge(S["weights"], N_LOADS * 16)
            turns = turns_of(sp)

            def base_of(st):
                return sp.value_load(step_row[0:1, 0, bass.ds(st.t, 1)], min_val=0, max_val=NPAD - GROUP)

            def group_rows(dram, base):
                return dram[bass.ds(base, GROUP), :].rearrange("(p t) d -> p (t d)", t=TILES)

            def entries_in(st):
                chunk = sp.value_load(step_row[0:1, 1, bass.ds(st.t, 1)], min_val=0, max_val=shared["CHUNKS"])
                after(sp, "idx", st, back=4)
                sp.sem_inc(S["go"], 1)
                after(sp, "oh", st, per=2, back=UN)
                after(sp, "idx", st, back=4)
                for k in range(2):
                    sp.dma_start(ent[:, st.slot(UN), k, :], lists[k][bass.ds(chunk * P, P), :]).then_inc(d_ent[st.slot(4)], 16)

            def h_in(st):
                base = base_of(st)
                after(sp, "tn", st, back=4)
                sp.sem_inc(S["go"], 1)
                after(sp, "sum", st, per=2, back=4)
                sp.dma_start(h_rows[:, st.slot(4), :], group_rows(h1_dram, base)).then_inc(d_h[st.slot(4)], 16)

            def x_in(st):
                base = base_of(st)
                after(sp, "out", st, back=4)
                sp.dma_start(x_rows[:, st.slot(4), :], group_rows(x1_dram, base)).then_inc(d_x[st.slot(4)], 16)

            def rows_out(st):
                base = base_of(st)
                after(sp, "out", st)
                landed(sp, d_out, st, back=1)
                sp.dma_start(group_rows(out, base), out_rows[:, st.slot(4), :]).then_inc(d_out[st.slot(2)], 16)

            loop(sp, turns, [(0, entries_in), (5, h_in), (11, x_in), (15, rows_out)])
            landed(sp, d_out, Step(turns, PEEL * UN - 1))
            sp.sem_inc(S["go"], 1)

        @block.gpsimd
        def _(pool):
            G_ = nc.gpsimd
            G_.iota(iota_loc[:, :, :], pattern=[[1, TILES], [TILES, P]], base=1, channel_multiplier=0,
                    allow_small_or_imprecise_dtypes=True).then_inc(S["const"], 1)
            G_.memset(ones_h[:, :], 1.0).then_inc(S["const"], 1)
            pool.wait_ge(S["prep"], 17 + 2 * TILES)
            G_.partition_all_reduce(wmax[:, 3:4], wmax[:, 2:3], P, RMAX).then_inc(S["const"], 1)
            turns = turns_of(pool)

            def gather(st):
                after(pool, "idx", st)
                after(pool, "high", st, back=4)
                after(pool, "low", st, back=4)
                pool.sem_inc(S["go"], 1)
                for k in range(2):
                    G_.indirect_dma_start(out=rows[:, st.slot(4), k, :], out_offset=None, in_=h1_dram[:, :],
                                          in_offset=bass.IndirectOffsetOnAxis(ap=idx[:, st.slot(4), k:k + 1], axis=0)
                                          ).then_inc(d_gat[st.slot(4)], 16)

            def low_part(st):
                after(pool, "high", st)
                after(pool, "agg", st, back=4)
                G_.tensor_tensor(part[:, st.slot(4), 1, :, :], rows[:, st.slot(4), :, :], part[:, st.slot(4), 0, :, :],
                                 ALU.subtract).then_inc(S["low"], 1)

            def blend(st):
                s2 = st.slot(2)
                after(pool, "n", st)
                after(pool, "e", st, back=2)
                G_.tensor_tensor(d[:, s2, :], hT[:, st.slot(UN), :], n[:, st.slot(4), :], ALU.subtract).then_inc(S["d"], 1)
                after(pool, "d", st)
                after(pool, "z", st)
                after(pool, "f", st, back=2)
                G_.tensor_tensor(e[:, s2, :], z[:, st.slot(4), :], d[:, s2, :], ALU.mult).then_inc(S["e"], 1)

            def low_h(st):
                after(pool, "hh", st)
                after(pool, "nhg", st, back=2)
                G_.tensor_tensor(hp[:, st.slot(2), 1, :], hT[:, st.slot(UN), :], hp[:, st.slot(2), 0, :], ALU.subtract).then_inc(S["hl"], 1)

            loop(pool, turns, [(12, blend), (8, low_h), (6, low_part), (3, gather)])

        @block.scalar
        def _(act):
            A = nc.scalar
            act.wait_ge(S["prep"], 25 + 2 * TILES)
            turns = turns_of(act)
            has_loops = act.value_load(looped_i[0:1, 0:1], min_val=0, max_val=1)

            def high_part(st):
                landed(act, d_gat, st, per=32)
                after(act, "agg", st, back=4)
                A.copy(part[:, st.slot(4), 0, :, :], rows[:, st.slot(4), :, :]).then_inc(S["high"], 1)

            def mean_columns(k):
                def stage(st):
                    after(act, f"tm{k}", st)
                    after(act, "nig", st, back=2)
                    if k == 1:
                        act.sem_inc(S["go"], 1)
                        with act.If(has_loops < 1):
                            A.copy(none[:, st.slot(2), :], ps_t[0:2 * TILES, GROUP:GROUP + P]).then_inc(S["none"], 1)
                    A.copy(mT[:, st.slot(2), k, 0, :], ps_t[:, 0:GROUP]).then_inc(S[f"mh{k}"], 1)
                return stage

            def reset_gate(st):
                after(act, "rg", st)
                after(act, "rh", st, back=2)
                A.activation(r[:, st.slot(2), :], ps_r[:, 0:GROUP], ACT.Sigmoid, bias=b_gate[:, 0:1], scale=unscale[:, :]).then_inc(S["r"], 1)

            def update_gate(st):
                after(act, "zg", st)
                after(act, "e", st, back=4)
                A.activation(z[:, st.slot(4), :], ps_z[:, 0:GROUP], ACT.Sigmoid, bias=b_gate[:, 1:2], scale=unscale[:, :]).then_inc(S["z"], 1)

            def candidate(st):
                after(act, "pre", st)
                after(act, "f", st, back=4)
                after(act, "d", st, back=4)
                A.activation(n[:, st.slot(4), :], pre[:, st.slot(2), :], ACT.Tanh, bias=b_gate[:, 2:3], scale=unscale[:, :]).then_inc(S["n"], 1)

            def columns(st):
                after(act, "tn", st)
                after(act, "d", st, back=UN)
                A.copy(hT[:, st.slot(UN), :], ps_t[:, 0:GROUP]).then_inc(S["hT"], 1)

            def high_h(st):
                after(act, "hT", st)
                after(act, "nhg", st, back=2)
                A.copy(hp[:, st.slot(2), 0, :], hT[:, st.slot(UN), :]).then_inc(S["hh"], 1)

            loop(act, turns, [(8, columns), (8, mean_columns(0)), (8, high_h), (11, candidate), (8, mean_columns(1)), (9, reset_gate), (9, update_gate), (5, high_part)])

        @block.tensor
        def _(pe):
            T = nc.tensor
            pe.wait_ge(S["weights"], N_LOADS * 16)
            for g in range(3):
                for side in range(2):
                    T.transpose((ps_r, ps_z)[side][:, g * D:(g + 1) * D], w_ih[:, g, side * D:(side + 1) * D], ident_f[:, :])
                mm = T.transpose(ps_nh[:, g * D:(g + 1) * D], w_hh[:, g, :], ident_f[:, :])
            mm.then_inc(S["turned"], 1)
            pe.wait_ge(S["wcopy"], 3)
            T.matmul(ps_s0[:, 0:H3], w_in[:, :], w_ihT[:, 0, :], start=True, stop=True)
            T.matmul(ps_s1[:, 0:H3], w_out[:, :], w_ihT[:, 1, :], start=True, stop=True)
            pe.wait_ge(S["prep"], 2 + 2 * TILES)
            for t, bank in enumerate((ps_ni, ps_t, ps_r)):
                for side in range(2):
                    T.matmul(bank[0:2 * TILES, 0:H3], c_pick[:, side, t, :], w_ihT[:, side, :], start=(side == 0), stop=(side == 1))
            for side in range(2):
                for g in range(3):
                    mm = T.matmul(ps_o[:, side * 3 + g:side * 3 + g + 1], w_ihT[:, side, g * D:(g + 1) * D], b_side[:, side:side + 1],
                                  start=True, stop=True)
            mm.then_inc(S["turned"], 1)
            pe.wait_ge(S["prep"], 25 + 2 * TILES)
            turns = turns_of(pe)
            has_loops = pe.value_load(looped_i[0:1, 0:1], min_val=0, max_val=1)

            def turn_h(st):
                landed(pe, d_h, st)
                after(pe, "ml1", st, back=1)
                for q in range(TILES):
                    mm = T.transpose(ps_t[:, q * P:(q + 1) * P], h_rows[:, st.slot(4), q * D:(q + 1) * D], ident_f[:, :])
                mm.then_inc(S["tn"], 1)

            def turn_mean(k):
                def stage(st):
                    if k == 0:
                        after(pe, "mean", st)
                        after(pe, "hT", st)
                    else:
                        after(pe, "ml0", st)
                    for q in range(TILES + k):
                        mm = T.transpose(ps_t[:, q * P:(q + 1) * P], mean[:, st.slot(2), (k * TILES + q) * D:(k * TILES + q + 1) * D], ident_f[:, :])
                    mm.then_inc(S[f"tm{k}"], 1)
                return stage

            def aggregate(st):
                after(pe, "low", st)
                after(pe, "oh", st, per=2)
                after(pe, "sum", st, per=2, back=1)
                after(pe, "edges", st, per=2, back=1)
                for k in range(2):
                    for t in range(TILES):
                        chosen = onehot[:, st.slot(2), k, t * P:(t + 1) * P]
                        for q in range(2):
                            T.matmul(ps_s[k][:, t * D:(t + 1) * D], chosen, part[:, st.slot(4), q, k, :], start=(q == 0), stop=(q == 1),
                                     skip_group_check=True)
                        mm = T.matmul(ps_s[k][:, GROUP + t:GROUP + t + 1], chosen, ones_h[:, :], start=True, stop=True, skip_group_check=True)
                mm.then_inc(S["agg"], 1)

            def gates(st, which):
                s2 = st.slot(2)
                moving = (mT[:, s2, 0, :, :], mT[:, s2, 1, :, :], hp[:, s2, :, :])

                def gate(bank, g, sides, name, corrected):
                    terms = [(side, wq, xq) for side in sides for wq, xq in ((0, 0), (1, 0), (0, 1))]
                    for q, (side, wq, xq) in enumerate(terms):
                        mm = T.matmul(bank[:, 0:GROUP], wp[:, wq, side, g * D:(g + 1) * D], moving[side][:, xq, :], start=(q == 0),
                                      stop=(q == len(terms) - 1), skip_group_check=corrected)
                        if corrected and q == 0:
                            for t in range(TILES):
                                T.matmul(bank[:, t * P:(t + 1) * P], c_rows[:, t, g * D:(g + 1) * D], none[:, s2, :],
                                         start=False, stop=False, skip_group_check=True)
                    mm.then_inc(S[name], 1)

                pe.sem_inc(S["go"], 1)
                with pe.If(has_loops > 0):
                    for bank, g, sides, name in which:
                        gate(bank, g, sides, name, False)
                with pe.Else():
                    after(pe, "none", st)
                    for bank, g, sides, name in which:
                        gate(bank, g, sides, name, 0 in sides)

            def gates_rh(st):
                for part in ("mh1", "ml1", "hl"):
                    after(pe, part, st)
                after(pe, "r", st, back=1)
                after(pe, "rh", st, back=1)
                gates(st, ((ps_r, 0, (0, 1, 2), "rg"), (ps_nh, 2, (2,), "nhg")))

            def gates_zn(st):
                after(pe, "z", st, back=1)
                after(pe, "pre", st, back=1)
                gates(st, ((ps_z, 1, (0, 1, 2), "zg"), (ps_ni, 2, (0, 1), "nig")))

            def turn_out(st):
                after(pe, "f", st)
                after(pe, "out", st, back=1)
                for q in range(3):
                    mm = T.transpose(ps_o[:, q * P:(q + 1) * P], f[:, st.slot(2), q * P:(q + 1) * P], ident_f[:, :])
                mm.then_inc(S["to"], 1)

            loop(pe, turns, [(8, turn_h), (7, aggregate), (8, turn_mean(0)), (14, turn_out), (9, gates_rh), (8, turn_mean(1)), (9, gates_zn)])

        @block.vector
        def _(v):
            V = nc.vector
            done = [0]

            def link(ins):
                done[0] += 1
                ins.then_inc(S["prep"], 1)
                v.wait_ge(S["prep"], done[0])

            v.wait_ge(S["weights"], N_LOADS * 16)
            v.wait_ge(S["const"], 2)
            link(V.memset(c_pick[:, :, :, :], 0.0))
            link(V.memset(mean[:, :, 2 * GROUP:2 * GROUP + P], 0.0))
            for k in range(2):
                for t in range(TILES):
                    link(V.tensor_scalar(c_pick[:, k, t, k * TILES + t:k * TILES + t + 1], b_side[:, k:k + 1], -1.0, None, ALU.mult))
            link(V.memset(edges[:, :, :, :], 0.0))
            link(V.memset(sums[:, :, :, :], 0.0))
            v.wait_ge(S["turned"], 1)
            V.tensor_copy(w_ihT[:, 0, :], ps_r[:, 0:H3]).then_inc(S["wcopy"], 1)
            V.tensor_copy(w_ihT[:, 1, :], ps_z[:, 0:H3]).then_inc(S["wcopy"], 1)
            V.tensor_copy(lhs[:, 2, :], ps_nh[:, 0:H3]).then_inc(S["wcopy"], 1)
            v.wait_ge(S["turned"], 2)
            V.tensor_copy(lhs[:, 0, :], ps_s0[:, 0:H3]).then_inc(S["wcopy"], 1)
            V.tensor_copy(lhs[:, 1, :], ps_s1[:, 0:H3]).then_inc(S["wcopy"], 1)
            for t, bank in enumerate((ps_ni, ps_t, ps_r)):
                V.tensor_copy(c_rows[:, t, :], bank[0:2 * TILES, 0:H3]).then_inc(S["wcopy"], 1)
            v.wait_ge(S["wcopy"], 5 + TILES)
            link(V.tensor_copy(c_gate[:, :, :], ps_o[:, 0:6].rearrange("p (s g) -> p s g", s=2)))
            link(V.tensor_tensor(c_sum[:, :], c_gate[:, 0, :], c_gate[:, 1, :], ALU.add))
            link(V.tensor_tensor(c_sum[:, :], c_sum[:, :], b_ih[:, :], ALU.add))
            link(V.tensor_tensor(b_gate[:, 0:2], c_sum[:, 0:2], b_hh[:, 0:2], ALU.add))
            link(V.tensor_copy(b_gate[:, 2:3], c_sum[:, 2:3]))
            link(V.tensor_copy(b_gate[:, 3:4], b_hh[:, 2:3]))
            link(V.tensor_copy(looped_i[:, :], looped[:, :]))
            link(V.tensor_reduce(wmax[:, 0:1], lhs[:, :, :].rearrange("p s h -> p (s h)"), AX, ALU.max))
            link(V.tensor_reduce(wmax[:, 1:2], lhs[:, :, :].rearrange("p s h -> p (s h)"), AX, ALU.min))
            link(V.scalar_tensor_tensor(out=wmax[:, 2:3], in0=wmax[:, 1:2], scalar=-1.0, in1=wmax[:, 0:1], op0=ALU.mult, op1=ALU.max))
            link(V.tensor_scalar(wmax[:, 2:3], wmax[:, 2:3], 1e-30, 1e30, ALU.max, ALU.min))
            link(V.memset(fresh[:, :, :], 0.0))
            link(V.memset(share[:, :, :, :], 0.0))
            v.wait_ge(S["const"], 3)
            link(V.tensor_scalar(wexp[:, :], wmax[:, 3:4].bitcast(I32), 0x7F800000, None, ALU.bitwise_and))
            link(V.tensor_scalar(unscale[:, :], wexp[:, :].bitcast(F32), 2.0 ** -13, None, ALU.mult))
            link(V.reciprocal(scale[:, :], unscale[:, :]))
            link(V.tensor_scalar(lhs[:, :, :], lhs[:, :, :], scale[:, :], None, ALU.mult))
            link(V.tensor_copy(wp[:, 0, :, :], lhs[:, :, :]))
            link(V.tensor_tensor(wp[:, 1, :, :], lhs[:, :, :], wp[:, 0, :, :], ALU.subtract))
            link(V.tensor_scalar(b_gate[:, 3:4], b_gate[:, 3:4], scale[:, :], None, ALU.mult))
            link(V.tensor_scalar(c_rows[:, :, :], c_rows[:, :, :], scale[0:2 * TILES, :], None, ALU.mult))
            turns = turns_of(v)
            rounds = v.value_load(rounds_i[0:1, 0:1], min_val=1, max_val=shared["ROUNDS"])

            def row_numbers(st):
                landed(v, d_ent, st, per=32)
                landed(v, d_gat, st, back=4, per=32)
                V.scalar_tensor_tensor(out=idx[:, st.slot(4), :], in0=ent[:, st.slot(UN), :, 0], scalar=256.0, in1=ent[:, st.slot(UN), :, 1],
                                       op0=ALU.mult, op1=ALU.add).then_inc(S["idx"], 1)

            def one_hots(st):
                after(v, "agg", st, back=2)
                for k in range(2):
                    V.tensor_scalar(onehot[:, st.slot(2), k, :], iota_loc[:, :, :].rearrange("p t r -> p (t r)"), ent[:, st.slot(UN), k, 2:3],
                                    None, ALU.is_equal).then_inc(S["oh"], 1)

            def add_sums(st):
                s2 = st.slot(2)
                after(v, "agg", st)
                after(v, "edges", st, per=2, back=1)
                for k in range(2):
                    V.scalar_tensor_tensor(out=edges[:, s2, k, :], in0=edges[:, 1 - s2, k, :], scalar=step_f[:, 1, bass.ds(st.t, 1)],
                                           in1=ps_s[k][:, GROUP:GROUP + TILES], op0=ALU.mult, op1=ALU.add).then_inc(S["edges"], 1)
                landed(v, d_h, st)
                after(v, "mean", st, back=2)
                v.sem_inc(S["go"], 1)

                def whole(out, scalar, k, name):
                    V.scalar_tensor_tensor(out=out, in0=h_rows[:, st.slot(4), :], scalar=scalar, in1=ps_s[k][:, 0:GROUP],
                                           op0=ALU.mult, op1=ALU.add).then_inc(S[name], 1)

                with v.If(rounds > 1):
                    after(v, "sum", st, per=2, back=1)
                    for k in range(2):
                        whole(fresh[:, k, :], step_f[:, 3, bass.ds(st.t, 1)], k, "fresh")
                    after(v, "fresh", st, per=2)
                    for k in range(2):
                        V.scalar_tensor_tensor(out=sums[:, s2, k, :], in0=sums[:, 1 - s2, k, :], scalar=step_f[:, 1, bass.ds(st.t, 1)],
                                               in1=fresh[:, k, :], op0=ALU.mult, op1=ALU.add).then_inc(S["sum"], 1)
                with v.Else():
                    for k in range(2):
                        whole(sums[:, s2, k, :], looped[:, :], k, "sum")

            def counts(st):
                s2 = st.slot(2)
                after(v, "edges", st, per=2)
                after(v, "tm1", st, back=2)
                V.tensor_scalar(count[:, s2, :, :], edges[:, s2, :, :], looped[:, :], 1.0, ALU.add, ALU.max).then_inc(S["count"], 1)
                V.tensor_scalar(mean[:, s2, 2 * GROUP:2 * GROUP + 2 * TILES], edges[:, s2, :, :].rearrange("p k t -> p (k t)"), 0.5, None,
                                ALU.is_lt).then_inc(S["count"], 1)

            def shares(st):
                after(v, "count", st, per=2)
                V.reciprocal(share[:, st.slot(2), :, :], count[:, st.slot(2), :, :]).then_inc(S["share"], 1)

            def means(st):
                s2 = st.slot(2)
                after(v, "share", st)
                after(v, "sum", st, per=2)
                V.tensor_tensor(mean[:, s2, 0:2 * GROUP].rearrange("p (k d) -> p k d", d=D),
                                sums[:, s2, :, :].rearrange("p k (t d) -> p (k t) d", d=D),
                                share[:, s2, :, :].rearrange("p k t -> p (k t)").unsqueeze(2).to_broadcast([P, 2 * TILES, D]),
                                ALU.mult).then_inc(S["mean"], 1)

            def reset_part(st):
                after(v, "r", st)
                after(v, "nhg", st)
                after(v, "pre", st, back=2)
                V.scalar_tensor_tensor(out=rh[:, st.slot(2), :], in0=ps_nh[:, 0:GROUP], scalar=b_gate[:, 3:4], in1=r[:, st.slot(2), :],
                                       op0=ALU.add, op1=ALU.mult).then_inc(S["rh"], 1)

            def mean_low(k):
                def stage(st):
                    after(v, f"mh{k}", st)
                    after(v, "nig", st, back=2)
                    V.tensor_tensor(mT[:, st.slot(2), k, 1, :], ps_t[:, 0:GROUP], mT[:, st.slot(2), k, 0, :], ALU.subtract).then_inc(S[f"ml{k}"], 1)
                return stage

            def before_tanh(st):
                after(v, "rh", st)
                after(v, "nig", st)
                after(v, "n", st, back=2)
                V.tensor_tensor(pre[:, st.slot(2), :], ps_ni[:, 0:GROUP], rh[:, st.slot(2), :], ALU.add).then_inc(S["pre"], 1)

            def new_h(st):
                after(v, "e", st)
                after(v, "to", st, back=2)
                V.tensor_tensor(f[:, st.slot(2), :], n[:, st.slot(4), :], e[:, st.slot(2), :], ALU.add).then_inc(S["f"], 1)

            def add_x(st):
                landed(v, d_x, st)
                after(v, "to", st)
                landed(v, d_out, st, back=4)
                V.tensor_tensor(out_rows[:, st.slot(4), :], x_rows[:, st.slot(4), :], ps_o[:, 0:GROUP], ALU.add).then_inc(S["out"], 1)

            loop(v, turns, [(10, before_tanh), (7, add_sums), (7, counts), (8, mean_low(0)), (13, new_h), (7, shares), (2, row_numbers), (6, one_hots),
                            (8, mean_low(1)), (14, add_x),
                            (7, means), (9, reset_part)])


def layout(x, src, dst):
    import numpy as np
    n, e = x.shape[0], src.shape[0]
    groups, cols, _, _ = sizes(n, e)
    x_pad = np.zeros(((groups + 1) * GROUP, D), x.dtype)
    x_pad[:n] = x
    src_pad = np.zeros(P * cols, src.dtype)
    src_pad[:e] = src
    dst_pad = np.full(P * cols + 1, 2 * n, dst.dtype)
    dst_pad[:e] = dst
    return {"x": x_pad, "src": src_pad, "dst": dst_pad}



def kernel(**inputs):
    import numpy as np
    import concourse.bacc as _bacc
    from concourse import mybir as _mybir
    from concourse.bass_utils import run_bass_kernel_spmd as _run

    x, src, dst = (np.ascontiguousarray(inputs[name]) for name in ("x", "src", "dst"))
    n_nodes, n_edges = x.shape[0], src.shape[0]
    arrays = layout(x, src, dst)
    for layer, names in (("L0_gnn_", ("W1", "b1", "W2", "b2")),
                         ("L1_gnn_", ("W_in", "b_in", "W_out", "b_out", "w_ih", "w_hh", "b_ih", "b_hh"))):
        for name in names:
            arrays[name] = np.ascontiguousarray(inputs[layer + name])

    nc = _bacc.Bacc("TRN2", target_bir_lowering=False, num_devices=1)
    ins = {name: nc.dram_tensor(f"in_{name}_dram", a.shape, _mybir.dt.from_np(a.dtype), kind="ExternalInput").ap()
           for name, a in arrays.items()}
    rows = (sizes(n_nodes, n_edges)[0] + 1) * GROUP
    out = nc.dram_tensor("out_0_dram", (rows, D), _mybir.dt.float32, kind="ExternalOutput").ap()
    build(nc, n_nodes, n_edges, ins["x"], ins["src"], ins["dst"], ins, out)
    r = _run(nc, [{f"in_{name}_dram": a for name, a in arrays.items()}], core_ids=[0])
    return r.results[0]["out_0_dram"][:n_nodes]
```
